# Optimizing a Trainium2 kernel written in Bass

```python
import numpy as np
import jax
import jax.numpy as jnp

def _softmax(x, axis=-1):
    return jax.nn.softmax(x, axis=axis)

def _gelu(x):
    return jax.nn.gelu(x, approximate=True)

def _silu(x):
    return jax.nn.silu(x)

def _sigmoid(x):
    return jax.nn.sigmoid(x)

def _layernorm(x, axis=-1, eps=1e-05):
    m = jnp.mean(x, axis=axis, keepdims=True)
    v = jnp.var(x, axis=axis, keepdims=True)
    return (x - m) / jnp.sqrt(v + eps)

def _scatter_add(tgt, idx, src, axis=0):
    return tgt.at[idx].add(src)

def _segment_sum(src, seg, n):
    return jax.ops.segment_sum(src, seg, n)
kernel_name = 'mk_xattn_seq_d1_seqx_r8_4af645'

def setup_inputs(seed: int=0):
    np.random.seed(seed)
    _w = jnp.asarray

    def _rec_inputs():
        import jax
        import jax.numpy as jnp
        _rk = jax.random.key(seed)
        x = -0.0002928 + 1 * jax.random.normal(jax.random.fold_in(_rk, 1), (4, 256, 256), jnp.float32)
        _lenS = 256 - jax.random.randint(jax.random.fold_in(_rk, 7), (4,), 0, max(1, 256 // 4) + 1, jnp.int32)
        _lenS2 = 256 - jax.random.randint(jax.random.fold_in(_rk, 8), (4,), 0, max(1, 256 // 4) + 1, jnp.int32)
        _ctx_2048P = jax.random.normal(jax.random.fold_in(_rk, 11), (4, 16, 256), jnp.float32)
        _ctx_2048c = jax.random.dirichlet(jax.random.fold_in(_rk, 511), 0.3 * jnp.ones((16,), jnp.float32), (4, 256))
        _ctx_2048t = jnp.einsum('bsk,bkd->bsd', _ctx_2048c, _ctx_2048P)
        _ctx_2048t = _ctx_2048t * jax.lax.rsqrt(jnp.mean(jnp.square(_ctx_2048t)) + 1e-12) * 0.953939
        ctx_2048 = -1.39393e-06 + 0.999914 * (_ctx_2048t + 0.3 * jax.random.normal(jax.random.fold_in(_rk, 611), (4, 256, 256), jnp.float32))
        _validS = jnp.arange(256)[None, :] < _lenS[:, None]
        _validS2 = jnp.arange(256)[None, :] < _lenS2[:, None]
        _causal = jnp.tril(jnp.ones((256, 256), dtype=bool))
        mask_1x1xSxS2_fc1 = jnp.where(jnp.broadcast_to(_validS2[0:1, None, None, :], (1, 1, 256, 256)), 1.0, 0.0).astype(jnp.float32)
        mask_Bx1xSxS2_ff1 = jnp.where(jnp.ones((4, 1, 256, 256), dtype=bool), 1.0, 0.0).astype(jnp.float32)
        return (x, ctx_2048, mask_1x1xSxS2_fc1, mask_Bx1xSxS2_ff1)
    x, ctx_2048, mask_1x1xSxS2_fc1, mask_Bx1xSxS2_ff1 = _rec_inputs()

    def _L0_xattn_setup():
        import jax, jax.numpy as jnp
        import numpy as np
        H = 256
        NH = 16
        HD = H // NH
        EPS = 1e-05

        def gelu(x):
            return 0.5 * x * (1.0 + jnp.tanh(0.7978845608028654 * x * (1.0 + 0.044715 * x * x)))

        def layernorm(x, scale, bias):
            m = jnp.mean(x, axis=-1, keepdims=True)
            v = jnp.mean(jnp.square(x - m), axis=-1, keepdims=True)
            return (x - m) * jax.lax.rsqrt(v + EPS) * scale + bias

        def split_heads(x):
            b, s, _ = x.shape
            return x.reshape(b, s, NH, HD).transpose(0, 2, 1, 3)

        def merge_heads(x):
            b, nh, s, hd = x.shape
            return x.transpose(0, 2, 1, 3).reshape(b, s, nh * hd)

        def attention(q, k, v, mask):
            scores = jnp.einsum('bhqd,bhkd->bhqk', q, k) / jnp.sqrt(jnp.float32(HD))
            scores = scores * mask - 10000.0 * (1.0 - mask)
            probs = jax.nn.softmax(scores, axis=-1)
            return jnp.einsum('bhqk,bhkd->bhqd', probs, v)
        key = jax.random.key(seed)
        ks = jax.random.split(key, 16)
        b, s, t = (2, 128, 128)
        w = lambda k, i, o: jax.random.normal(k, (i, o), jnp.float32) * 0.02
        inp = {'hidden_states': jax.random.normal(ks[0], (b, s, H), jnp.float32), 'encoder_states': jax.random.normal(ks[1], (b, t, H), jnp.float32), 'ltor_mask': jnp.tril(jnp.ones((1, 1, s, s), jnp.float32)), 'cross_mask': jnp.ones((b, 1, s, t), jnp.float32), 'ln1_s': jnp.ones((H,), jnp.float32), 'ln1_b': jnp.zeros((H,), jnp.float32), 'w_qkv': w(ks[2], H, 3 * H), 'b_qkv': jnp.zeros((3 * H,), jnp.float32), 'w_ao': w(ks[3], H, H), 'b_ao': jnp.zeros((H,), jnp.float32), 'ln2_s': jnp.ones((H,), jnp.float32), 'ln2_b': jnp.zeros((H,), jnp.float32), 'w_q': w(ks[4], H, H), 'b_q': jnp.zeros((H,), jnp.float32), 'w_kv': w(ks[5], H, 2 * H), 'b_kv': jnp.zeros((2 * H,), jnp.float32), 'w_co': w(ks[6], H, H), 'b_co': jnp.zeros((H,), jnp.float32), 'ln3_s': jnp.ones((H,), jnp.float32), 'ln3_b': jnp.zeros((H,), jnp.float32), 'w1': w(ks[7], H, 4 * H), 'b1': jnp.zeros((4 * H,), jnp.float32), 'w2': w(ks[8], 4 * H, H), 'b2': jnp.zeros((H,), jnp.float32)}
        return inp
    _L0_xattn_all = _L0_xattn_setup()
    _L0_xattn_in = {k: v for k, v in _L0_xattn_all.items() if k in ('ln1_s', 'ln1_b', 'w_qkv', 'b_qkv', 'w_ao', 'b_ao', 'ln2_s', 'ln2_b', 'w_q', 'b_q', 'w_kv', 'b_kv', 'w_co', 'b_co', 'ln3_s', 'ln3_b', 'w1', 'b1', 'w2', 'b2')}
    del _L0_xattn_all
    return {'x': x, 'ctx_2048': ctx_2048, 'mask_1x1xSxS2_fc1': mask_1x1xSxS2_fc1, 'mask_Bx1xSxS2_ff1': mask_Bx1xSxS2_ff1, 'L0_xattn_ln1_s': _L0_xattn_in['ln1_s'], 'L0_xattn_ln1_b': _L0_xattn_in['ln1_b'], 'L0_xattn_w_qkv': _L0_xattn_in['w_qkv'], 'L0_xattn_b_qkv': _L0_xattn_in['b_qkv'], 'L0_xattn_w_ao': _L0_xattn_in['w_ao'], 'L0_xattn_b_ao': _L0_xattn_in['b_ao'], 'L0_xattn_ln2_s': _L0_xattn_in['ln2_s'], 'L0_xattn_ln2_b': _L0_xattn_in['ln2_b'], 'L0_xattn_w_q': _L0_xattn_in['w_q'], 'L0_xattn_b_q': _L0_xattn_in['b_q'], 'L0_xattn_w_kv': _L0_xattn_in['w_kv'], 'L0_xattn_b_kv': _L0_xattn_in['b_kv'], 'L0_xattn_w_co': _L0_xattn_in['w_co'], 'L0_xattn_b_co': _L0_xattn_in['b_co'], 'L0_xattn_ln3_s': _L0_xattn_in['ln3_s'], 'L0_xattn_ln3_b': _L0_xattn_in['ln3_b'], 'L0_xattn_w1': _L0_xattn_in['w1'], 'L0_xattn_b1': _L0_xattn_in['b1'], 'L0_xattn_w2': _L0_xattn_in['w2'], 'L0_xattn_b2': _L0_xattn_in['b2']}

def reference(x, ctx_2048, mask_1x1xSxS2_fc1, mask_Bx1xSxS2_ff1, L0_xattn_ln1_s, L0_xattn_ln1_b, L0_xattn_w_qkv, L0_xattn_b_qkv, L0_xattn_w_ao, L0_xattn_b_ao, L0_xattn_ln2_s, L0_xattn_ln2_b, L0_xattn_w_q, L0_xattn_b_q, L0_xattn_w_kv, L0_xattn_b_kv, L0_xattn_w_co, L0_xattn_b_co, L0_xattn_ln3_s, L0_xattn_ln3_b, L0_xattn_w1, L0_xattn_b1, L0_xattn_w2, L0_xattn_b2):
    import jax
    import jax.numpy as jnp

    def _L0_xattn_ref(hidden_states, encoder_states, ltor_mask, cross_mask, ln1_s, ln1_b, w_qkv, b_qkv, w_ao, b_ao, ln2_s, ln2_b, w_q, b_q, w_kv, b_kv, w_co, b_co, ln3_s, ln3_b, w1, b1, w2, b2):
        import jax, jax.numpy as jnp
        import numpy as np
        H = 256
        NH = 16
        HD = H // NH
        EPS = 1e-05

        def gelu(x):
            return 0.5 * x * (1.0 + jnp.tanh(0.7978845608028654 * x * (1.0 + 0.044715 * x * x)))

        def layernorm(x, scale, bias):
            m = jnp.mean(x, axis=-1, keepdims=True)
            v = jnp.mean(jnp.square(x - m), axis=-1, keepdims=True)
            return (x - m) * jax.lax.rsqrt(v + EPS) * scale + bias

        def split_heads(x):
            b, s, _ = x.shape
            return x.reshape(b, s, NH, HD).transpose(0, 2, 1, 3)

        def merge_heads(x):
            b, nh, s, hd = x.shape
            return x.transpose(0, 2, 1, 3).reshape(b, s, nh * hd)

        def attention(q, k, v, mask):
            scores = jnp.einsum('bhqd,bhkd->bhqk', q, k) / jnp.sqrt(jnp.float32(HD))
            scores = scores * mask - 10000.0 * (1.0 - mask)
            probs = jax.nn.softmax(scores, axis=-1)
            return jnp.einsum('bhqk,bhkd->bhqd', probs, v)
        ln_out = layernorm(hidden_states, ln1_s, ln1_b)
        qkv = ln_out @ w_qkv + b_qkv
        q, k, v = jnp.split(qkv, 3, axis=-1)
        ctx = merge_heads(attention(split_heads(q), split_heads(k), split_heads(v), ltor_mask))
        attn_out = ctx @ w_ao + b_ao
        x = hidden_states + attn_out
        ln_out = layernorm(x, ln2_s, ln2_b)
        q = ln_out @ w_q + b_q
        kv = encoder_states @ w_kv + b_kv
        k, v = jnp.split(kv, 2, axis=-1)
        ctx = merge_heads(attention(split_heads(q), split_heads(k), split_heads(v), cross_mask))
        cross_out = ctx @ w_co + b_co
        x = x + cross_out
        ln_out = layernorm(x, ln3_s, ln3_b)
        mlp_out = gelu(ln_out @ w1 + b1) @ w2 + b2
        return x + mlp_out
    x = _L0_xattn_ref(x, ctx_2048, mask_1x1xSxS2_fc1, mask_Bx1xSxS2_ff1, L0_xattn_ln1_s, L0_xattn_ln1_b, L0_xattn_w_qkv, L0_xattn_b_qkv, L0_xattn_w_ao, L0_xattn_b_ao, L0_xattn_ln2_s, L0_xattn_ln2_b, L0_xattn_w_q, L0_xattn_b_q, L0_xattn_w_kv, L0_xattn_b_kv, L0_xattn_w_co, L0_xattn_b_co, L0_xattn_ln3_s, L0_xattn_ln3_b, L0_xattn_w1, L0_xattn_b1, L0_xattn_w2, L0_xattn_b2)
    return x

_drawn_inputs = setup_inputs


def setup_inputs(seed=0):
    import zlib

    import numpy as np

    out = dict(_drawn_inputs(seed))
    spreads = {'L0_xattn_ln1_s': (1.0, 0.6),
     'L0_xattn_ln1_b': (0.0, 0.766),
     'L0_xattn_b_qkv': (0.0, 0.272),
     'L0_xattn_b_ao': (0.0, 0.1),
     'L0_xattn_ln2_s': (1.0, 0.6),
     'L0_xattn_ln2_b': (0.0, 2.0),
     'L0_xattn_b_q': (0.0, 2.0),
     'L0_xattn_b_kv': (0.0, 0.283),
     'L0_xattn_b_co': (0.0, 0.1),
     'L0_xattn_ln3_s': (1.0, 0.6),
     'L0_xattn_ln3_b': (0.0, 0.654),
     'L0_xattn_b1': (0.0, 0.308),
     'L0_xattn_b2': (0.0, 0.1)}
    factors = {'L0_xattn_w_qkv': 4.658, 'L0_xattn_w_q': 8.0}
    for name, (base, spread) in spreads.items():
        noise = np.random.default_rng([zlib.crc32(name.encode()), seed]).standard_normal(out[name].shape)
        drawn = base * np.exp(spread * noise) if base else spread * noise
        out[name] = jnp.asarray(drawn.astype(out[name].dtype))
    for name, factor in factors.items():
        out[name] = (out[name] * factor).astype(out[name].dtype)
    return out
```

```python
from contextlib import ExitStack

import concourse.bass as bass
from concourse import mybir

F32 = mybir.dt.float32
F32R = mybir.dt.float32r
I32 = mybir.dt.int32
ALU = mybir.AluOpType
ACT = mybir.ActivationFunctionType
AX = mybir.AxisListType

NB, S, D, NH = 4, 256, 256, 16
HD = D // NH
FF = 4 * D
P = 128
TT = S // P
KC = D // P
FC = FF // P
EPS = 1e-5
SCORE_SCALE = HD ** -0.5
BIAS = 10000.0 * HD ** 0.5
UNITS = 2 * NB
HALVES = 2 * UNITS
HH = NH // 2
CHUNKS = 8 * HALVES
GROUPS = 4 * UNITS
LEAD = 13
RING = 3
ROWS_A, ROWS_B, CROW = 50, 65, 64
MLP0 = 8 * HALVES
PIECES = NB * FC // 2


def up_step(m):
    return MLP0 + m + (m >= 6)


def side_plan():
    plan = {}

    def put(t, kind, u):
        plan.setdefault(t, []).append((kind, u))

    put(-31, "cols", 0)
    put(-28, "flags", 0)
    put(-14, "flags", 1)
    for u in range(UNITS):
        t = 16 * u
        if u < NB:
            put(t - 29, "xT", u)
            put(t - 26, "q", u)
            put(t - 24, "k", u)
            put(t + 30, "xT2", u)
        else:
            put(t - 29, "eT", u)
            put(t - 26, "q", u)
            put(t - 24, "k", u)
        put(t - 14, "v", u)
        put(t - 4, "maxT", 2 * u)
        put(t + 4, "maxT", 2 * u + 1)
        put(t + 21, "ctxT", u)
        put(t + 24, "o", u)
    for b, t in enumerate((100, 108, 132, 139)):
        put(t, "xT3", b)
    for m in range(PIECES):
        put(up_step(m), "up", m)
    return plan


SIDE = side_plan()
FIRST_STEP = -34
LAST_STEP = up_step(PIECES - 1) + 4
DOWN = {up_step(m) + 3: m for m in range(PIECES)}
FINISH = {up_step(4 * b + 3) + 4: b for b in range(NB)}
LOT = 1024
SIDE_ORDER = [x for t in sorted(SIDE) for x in SIDE[t]]
NORMS = [x for x in SIDE_ORDER if x[0] in ("xT", "xT2", "xT3")]


def stats_step(kind, b):
    return {"xT": 16 * b - 33, "xT2": 16 * b + 25, "xT3": 16 * (b + NB) + 25}[kind]


STATS = {}
for _kind, _b in NORMS:
    STATS.setdefault(stats_step(_kind, _b), []).append((_kind, _b))


def side_slot(kind, u):
    j = SIDE_ORDER.index((kind, u))
    return j % 2, j // 2


def norm_index(kind, b):
    return NORMS.index((kind, b))


def decoder_layer(nc, x, ctx_in, self_mask, cross_mask, ln1_s, ln1_b, w_qkv, b_qkv, w_ao, b_ao,
                  ln2_s, ln2_b, w_q, b_q, w_kv, b_kv, w_co, b_co, ln3_s, ln3_b, w1, b1, w2, b2, out):
    with ExitStack() as stack:
        def sb(name, shape, dt=F32):
            return stack.enter_context(nc.sbuf_tensor(name, shape, dt))

        def ps(name, shape):
            return stack.enter_context(nc.psum_tensor(name, shape, F32))

        def sem(name):
            return stack.enter_context(nc.semaphore(name))

        def dram(name, shape):
            return nc.dram_tensor(name, shape, F32, kind="Internal").ap()

        q_scr = dram("q_scr", (UNITS, 2, NH, HD, S))
        k_scr = dram("k_scr", (UNITS, 2, NH, HD, S))
        bias_scr = dram("bias_scr", (1 + NB, 2, S))
        max_scr = dram("max_scr", (HALVES, HH, S))

        X = sb("X", [P, NB, TT, D])
        E = sb("E", [P, TT, D])
        WQKV = [sb(f"WQKV{i}", [P, KC, 3 * D], F32R) for i in range(2)]
        WAO = [sb(f"WAO{i}", [P, KC, D], F32R) for i in range(2)]
        WQ = [sb(f"WQ{i}", [P, KC, D], F32R) for i in range(2)]
        WKV = [sb(f"WKV{i}", [P, KC, 2 * D], F32R) for i in range(2)]
        WCO = [sb(f"WCO{i}", [P, KC, D], F32R) for i in range(2)]
        W1 = [sb(f"W1{i}", [P, KC, FF], F32R) for i in range(2)]
        W2 = [sb(f"W2{i}", [P, FC, D], F32R) for i in range(2)]
        QS = sb("QS", [P, RING, HH, S], F32R)
        KS = sb("KS", [P, RING, HH, S], F32R)
        HID = [KS[:, 1], QS[:, 1]]
        PR = sb("PR", [P, 2, 2, 4, S])
        RAW = PR[:].rearrange("p a b c n -> p (a b c n)")
        RAWQKV = RAW[:, 0:KC * 3 * D].rearrange("p (c n) -> p c n", c=KC)
        MK = RAW[:, KC * 3 * D:4096].rearrange("p (j t n) -> p j t n", j=1 + NB, t=TT)
        STG = sb("STG", [P, LOT])
        CB = sb("CB", [P, HH, S])
        V = sb("V", [P, 2, TT, NH, 2 * HD])
        XN = sb("XN", [P, TT, D])
        XT32 = sb("XT32", [P, KC, S])
        XS = [sb(f"XS{i}", [P, KC, S], F32R) for i in range(2)]
        XC = [sb(f"XC{i}", [P, KC, S], F32R) for i in range(2)]
        QX = sb("QX", [P, 2, 2, S], F32R)
        KX = sb("KX", [P, 2, 2, S], F32R)
        K32 = sb("K32", [P, 2, S])
        O32 = sb("O32", [P, S])
        RC = sb("RC", [P, 2, TT * 4])
        CT = sb("CT", [P, TT, D])
        CX = [sb(f"CX{i}", [P, KC, S], F32R) for i in range(2)]
        G32 = V[:, 0].rearrange("p t h d -> p (t h d)").rearrange("p (a n) -> p a n", a=2)
        MBI = sb("MBI", [P, 2, S])
        BF = CB[0:1, 4:8, :]
        BH = [KS[0:1, 2, 0:2, :].rearrange("p (j l) n -> p j l n", j=1),
              QS[0:1, 2, 0:2 * NB, :].rearrange("p (j l) n -> p j l n", j=NB)]
        MB = sb("MB", [P, 1 + NB, S])
        MG = sb("MG", [P, TT, S])
        MGT = sb("MGT", [P, TT, S])
        DIF = sb("DIF", [P, 1 + NB])
        FLG = sb("FLG", [P, 1 + NB])
        FLR = sb("FLR", [P, 1 + NB])
        MX = sb("MX", [P, 2, TT, HH])
        CR = sb("CR", [HH, 2, S], F32R)
        CG = sb("CG", [HH, S])
        ROWV = CB[0:32, 0, 0:P]
        COLV = sb("COLV", [P, 32])
        BV = sb("BV", [P, 2, D])
        BO = sb("BO", [P, 3, D])
        IDN = sb("IDN", [P, P])
        ONE = CB[:, 1, 0:P]
        ST = sb("ST", [P, 2, TT, 6])
        MV = sb("MV", [P, 2, TT, 2])
        RS = sb("RS", [P, 2, TT])
        NEGH = sb("NEGH", [P, TT])

        vecs = [(ln1_s, 2), (ln1_b, 2), (b_qkv, 4), (ln2_s, 2), (ln2_b, 2), (b_q, 2), (b_kv, 2),
                (ln3_s, 2), (ln3_b, 2), (b1, 8)]
        col = [sum(n for _, n in vecs[:i]) for i in range(len(vecs))]
        NV = sum(n for _, n in vecs)
        C_NORM = {"xT": (col[0], col[1]), "xT2": (col[3], col[4]), "xT3": (col[7], col[8])}
        C_Q, C_K, C_B1 = (col[2], col[5]), (col[2] + 2, col[6]), col[9]

        PA = ps("PA", [P, 2, 512])
        PB = ps("PB", [P, 2, 512])
        PV = ps("PV", [P, 2, 512])
        PSD = ps("PSD", [P, 2, 512])

        x_in = [sem(f"x_in{b}") for b in range(NB)]
        e_in, vec_in, bvec_in = sem("e_in"), sem("vec_in"), sem("bvec_in")
        wqkv_in, mask0_in, masks_in, stg_in = sem("wqkv_in"), sem("mask0_in"), sem("masks_in"), sem("stg_in")
        stg_high, stg_low, wqkv_split = sem("stg_high"), sem("stg_low"), sem("wqkv_split")
        id_zero, const_ready, stack_set, v_ones = sem("id_zero"), sem("const_ready"), sem("stack_set"), sem("v_ones")
        cols_ready, flags_ready, bias_ready = sem("cols_ready"), sem("flags_ready"), sem("bias_ready")
        bias_out, mask_step, mask_dif, flag_step = sem("bias_out"), sem("mask_step"), sem("mask_dif"), sem("flag_step")
        stats_ready, mv_ready = sem("stats_ready"), sem("mv_ready")
        rstd_step, rstd_ready = sem("rstd_step"), sem("rstd_ready")
        xn_ready, resid_ready = sem("xn_ready"), sem("resid_ready")
        xt32_ready, xt_high, xt_low = sem("xt32_ready"), sem("xt_high"), sem("xt_low")
        e_high, e_low, q_high, q_low = sem("e_high"), sem("e_low"), sem("q_high"), sem("q_low")
        k32_ready, k_high, k_low, v_ready = sem("k32_ready"), sem("k_high"), sem("k_low"), sem("v_ready")
        q_out, k_out = sem("q_out"), sem("k_out")
        stacked = [sem(f"stacked{r}") for r in range(RING)]
        side_filled = [sem(f"side_filled{i}") for i in range(2)]
        a_ready, max_done, crow_ready, crow_in = sem("a_ready"), sem("max_done"), sem("crow_ready"), sem("crow_in")
        b_ready, exp_done, pv_done, o_ready = sem("b_ready"), sem("exp_done"), sem("pv_done"), sem("o_ready")
        ot_done, recip_done, ctx_done = sem("ot_done"), sem("recip_done"), sem("ctx_done")
        cx_high, cx_low, o_added = sem("cx_high"), sem("cx_low"), sem("o_added")
        gelu_done, hid_high, hid_low, down_done = sem("gelu_done"), sem("hid_high"), sem("hid_low"), sem("down_done")
        fin_done, out_done = sem("fin_done"), sem("out_done")
        g_mask_in = [sem(f"g_mask_in{u}") for u in range(UNITS)]
        g_max_ready = [sem(f"g_max_ready{u}") for u in range(UNITS)]
        g_max_out = [sem(f"g_max_out{u}") for u in range(UNITS)]
        g_bcast_in = [sem(f"g_bcast_in{u}") for u in range(UNITS)]
        g_fixed = [sem(f"g_fixed{u}") for u in range(UNITS)]
        g_step_a = [sem(f"g_step_a{u}") for u in range(UNITS)]
        g_step_b = [sem(f"g_step_b{u}") for u in range(UNITS)]

        def mask_of(u):
            return 0 if u < NB else 1 + u - NB

        def mask_dram(j):
            return self_mask[0, 0] if j == 0 else cross_mask[j - 1, 0]

        def flags_count(u):
            return 1 if u < NB else 2

        def stack_dmas(s):
            return 7 if s < RING or s >= 2 * NB else 6

        def stack_count(s):
            return 16 * sum(stack_dmas(i) for i in range(s % RING, s + 1, RING))

        def filled(kind, u):
            bank, n = side_slot(kind, u)
            return side_filled[bank], n + 1

        def drained(kind, u):
            return {
                "cols": lambda: (cols_ready, 1),
                "flags": lambda: (flag_step, 5 * u + 1),
                "xT": lambda: (xt32_ready, norm_index(kind, u) + 1),
                "xT2": lambda: (xt32_ready, norm_index(kind, u) + 1),
                "xT3": lambda: (xt32_ready, norm_index(kind, u) + 1),
                "eT": lambda: (e_low, u - NB + 1),
                "q": lambda: (q_low, u + 1),
                "k": lambda: (k32_ready, u + 1),
                "v": lambda: (v_ready, u + 1),
                "maxT": lambda: (crow_ready, u + 1),
                "ctxT": lambda: (cx_low, u + 1),
                "o": lambda: (o_added, u + 1),
                "up": lambda: (gelu_done, u + 1),
            }[kind]()

        def norm_dst(kind, b):
            if kind == "xT":
                return XS
            if kind == "xT2":
                return XC
            return (XS, XC)[b % 2]

        def norm_dst_used(kind, b):
            if kind == "xT":
                return ("v", b - 1) if b else None
            if kind == "xT2":
                return ("q", NB + b - 1) if b else None
            return (("v", UNITS - 1), ("q", UNITS - 1), ("up", 3), ("up", 7))[b]

        def flat(w, lo, hi):
            return [t[:].rearrange("p c n -> p (c n)")[:, lo:hi] for t in w]

        PARTS = []
        for lot, pieces in enumerate(([(WAO, 0, 512), (WQ, 0, 512)], [(WKV, 0, 1024)], [(W1, 0, 1024)],
                                      [(W1, 1024, 2048)], [(W2, 0, 1024)], [(W2, 1024, 2048)], [(WCO, 0, 512)])):
            o = 0
            for w, lo, hi in pieces:
                for c in range(lo, hi, 512):
                    PARTS.append((flat(w, c, c + 512), o, lot))
                    o += 512
        SPLIT_STEPS = [-12, -11, -3, -2, 10, 11, 20, 22, 28, 29, 36, 37, 44]

        def parts_before(lot):
            return sum(1 for p in PARTS if p[2] < lot)

        W_AO_DONE, W_QUERY_DONE, W_KV_DONE, W_MLP_DONE, W_CO_DONE = 1, 2, 4, 12, 13

        block = stack.enter_context(nc.Block())

        @block.sync
        def _(sp):
            def load(dst, src, s):
                sp.dma_start(dst, src).then_inc(s, 16)

            def rows(ap):
                return ap.rearrange("(c p) n -> p c n", p=P)

            def load_lot(lot):
                if lot:
                    sp.wait_ge(stg_low, parts_before(lot))
                halves = [STG[:, 0:512].rearrange("p (c n) -> p c n", c=KC),
                          STG[:, 512:1024].rearrange("p (c n) -> p c n", c=KC)]
                if lot == 0:
                    load(halves[0], rows(w_ao), stg_in)
                    load(halves[1], rows(w_q), stg_in)
                elif lot == 1:
                    load(STG[:].rearrange("p (c n) -> p c n", c=KC), rows(w_kv), stg_in)
                elif lot in (2, 3):
                    load(STG[:], w1[(lot - 2) * P:(lot - 1) * P, :], stg_in)
                elif lot in (4, 5):
                    load(STG[:].rearrange("p (c n) -> p c n", c=4), rows(w2[(lot - 4) * 4 * P:(lot - 3) * 4 * P, :]), stg_in)
                else:
                    load(halves[0], rows(w_co), stg_in)

            load(X[:, 0], x[0].rearrange("(t p) d -> p t d", p=P), x_in[0])
            load(RAWQKV, rows(w_qkv), wqkv_in)
            load(MB[:, 0, :], self_mask[0, 0, 0, :].partition_broadcast(P), mask0_in)
            load(MK[:, 0], self_mask[0, 0].rearrange("(t p) n -> p t n", p=P), mask0_in)
            load(X[:, 1], x[1].rearrange("(t p) d -> p t d", p=P), x_in[1])
            load_lot(0)
            load(MB[:, 1:], cross_mask[:, 0, 0, :].partition_broadcast(P), masks_in)
            load(MK[:, 1:], cross_mask[:, 0].rearrange("b (t p) n -> p (b t) n", p=P).rearrange(
                "p (b t) n -> p b t n", t=TT), masks_in)
            for b in (2, 3):
                load(X[:, b], x[b].rearrange("(t p) d -> p t d", p=P), x_in[b])
            load(E[:], ctx_in[0].rearrange("(t p) d -> p t d", p=P), e_in)
            sp.wait_ge(bias_ready, 1)
            load(bias_scr[0:1], BH[0].bitcast(F32), bias_out)

            def write_qk(u):
                sp.wait_ge(q_high, u + 1)
                sp.wait_ge(q_low, u + 1)
                load(q_scr[u].rearrange("l (t h) d n -> (h d) (l t) n", t=2),
                     QX[:].bitcast(F32).rearrange("p l t n -> p (l t) n"), q_out)
                sp.wait_ge(k_high, u + 1)
                sp.wait_ge(k_low, u + 1)
                load(k_scr[u].rearrange("l (t h) d n -> (h d) (l t) n", t=2),
                     KX[:].bitcast(F32).rearrange("p l t n -> p (l t) n"), k_out)

            def load_stack(s):
                u, r, h0 = s // 2, s % RING, HH * (s % 2)
                if s < RING:
                    sp.wait_ge(stack_set, 3 * (s + 1))
                else:
                    sp.wait_ge(b_ready, 8 * (s - RING + 1))
                for dst, scr, parts, s_out in ((QS, q_scr, (0, 0, 1), q_out), (KS, k_scr, (0, 1, 0), k_out)):
                    sp.wait_ge(s_out, 16 * (u + 1))
                    for i, part in enumerate(parts):
                        load(dst[HD * i:HD * (i + 1), r].bitcast(F32),
                             scr[u, part, h0:h0 + HH].rearrange("h d n -> d h n"), stacked[r])
                if stack_dmas(s) == 7:
                    j = mask_of(u)
                    sp.wait_ge(bias_out, 16 if j == 0 else 32)
                    load(KS[3 * HD:3 * HD + 2, r].bitcast(F32),
                         bias_scr[j].unsqueeze(1).broadcast_to([2, HH, S]), stacked[r])

            flag = sp.alloc_register("sp_flag")

            def masks_by_query(u):
                j = mask_of(u)
                sp.wait_ge(flags_ready, flags_count(u))
                sp.reg_load(flag, FLG[0:1, j:j + 1].bitcast(I32))
                with sp.If_ne(flag, 0):
                    if u:
                        sp.wait_ge(max_done, 16 * u)
                    load(MG[:], mask_dram(j).rearrange("(t p) n -> p t n", p=P), g_mask_in[u])

            def write_max_row(s):
                u, r, n = s // 2, s % RING, s % 2
                sp.wait_ge(crow_ready, s + 1)
                load(QS[CROW:CROW + 1, r].bitcast(F32), CR[:, n, :].bitcast(F32), crow_in)
                j = mask_of(u)
                sp.reg_load(flag, FLG[0:1, j:j + 1].bitcast(I32))
                with sp.If_ne(flag, 0):
                    sp.wait_ge(g_max_ready[u], n + 1)
                    load(max_scr[s], CG[:, :], g_max_out[u])
                    sp.wait_ge(g_max_out[u], 16 * (n + 1))
                    if s:
                        sp.wait_ge(exp_done, 8 * s)
                    load(CB[:], max_scr[s].partition_broadcast(P), g_bcast_in[u])
                    if n == 0:
                        with nc.allow_non_contiguous_dma(reason="transposed mask, only on this path"):
                            for t in range(TT):
                                load(MGT[:, t], mask_dram(j)[:, t * P:(t + 1) * P].rearrange("q p -> p q"), g_mask_in[u])

            for s in range(HALVES):
                if s == 2:
                    sp.wait_ge(bias_ready, 2)
                    load(bias_scr[1:], BH[1].bitcast(F32), bias_out)
                    sp.wait_ge(bias_out, 32)
                if s % 2 == 0:
                    write_qk(s // 2)
                    masks_by_query(s // 2)
                load_stack(s)
                if s in (8, 10, 12):
                    u = s // 2
                    f, n = filled("eT", u)
                    sp.wait_ge(f, n)
                    load(E[:], ctx_in[u - NB + 1].rearrange("(t p) d -> p t d", p=P), e_in)
                if s:
                    write_max_row(s - 1)
                if 1 <= s <= 6:
                    load_lot(s)
            write_max_row(HALVES - 1)
            for b in range(NB):
                sp.wait_ge(fin_done, b + 1)
                load(out[b].rearrange("(t p) d -> p t d", p=P), X[:, b], out_done)
            sp.wait_ge(out_done, 16 * NB)

        @block.gpsimd
        def _(pool):
            pool.memset(IDN[:], 0.0).then_inc(id_zero, 1)
            pool.wait_ge(id_zero, 1)
            pool.affine_select(out=IDN[:], in_=IDN[:], compare_op=ALU.not_equal, fill=1.0, base=0,
                               pattern=[[-1, P]], channel_multiplier=1).then_inc(const_ready, 1)
            pool.memset(NEGH[:], -0.5).then_inc(const_ready, 1)
            pool.memset(ONE, 1.0).then_inc(const_ready, 1)

            def set_stack(r):
                pool.memset(QS[32:64, r].bitcast(F32), 1.0).then_inc(stack_set, 1)
                pool.wait_ge(stack_set, 3 * r + 1)
                pool.memset(KS[32:64, r].bitcast(F32), 0.0).then_inc(stack_set, 1)
                pool.wait_ge(stack_set, 3 * r + 2)
                pool.memset(KS[CROW:CROW + 1, r].bitcast(F32), 1.0).then_inc(stack_set, 1)
                pool.wait_ge(stack_set, 3 * r + 3)

            def rstd(n):
                pool.wait_ge(mv_ready, n + 1)
                if n == 0:
                    pool.wait_ge(const_ready, 3)
                if n >= 2:
                    pool.wait_ge(xn_ready, n - 1)
                r = RS[:, n % 2, :]
                pool.tensor_scalar(r, MV[:, n % 2, :, 1], 1.0, EPS, ALU.mult, ALU.add).then_inc(rstd_step, 1)
                pool.wait_ge(rstd_step, n + 1)
                pool.tensor_tensor(r, r, NEGH[:], ALU.pow).then_inc(rstd_ready, 1)

            def residual_bias(kind, b):
                n = norm_index(kind, b)
                pool.wait_ge(xn_ready, n + 1)
                if n == 0:
                    pool.wait_ge(bvec_in, 16 * 5)
                bias = BO[:, {"xT": 0, "xT2": 1, "xT3": 2}[kind], :].unsqueeze(1).broadcast_to([P, TT, D])
                pool.tensor_tensor(X[:, b], X[:, b], bias, ALU.add).then_inc(resid_ready, 1)

            def low_of_norm(kind, b):
                dst = norm_dst(kind, b)
                pool.wait_ge(xt_high, norm_index(kind, b) + 1)
                pool.tensor_tensor(dst[1][:], XT32[:], dst[0][:].bitcast(F32), ALU.subtract).then_inc(xt_low, 1)

            def low_of_keys(u):
                pool.wait_ge(k_high, u + 1)
                pool.tensor_tensor(KX[:, 1], K32[:], KX[:, 0].bitcast(F32), ALU.subtract).then_inc(k_low, 1)

            pool.wait_ge(const_ready, 3)
            set_stack(0)
            for t in range(FIRST_STEP, LAST_STEP + 1):
                for kind, b in STATS.get(t, ()):
                    rstd(norm_index(kind, b))
                for kind, u in SIDE.get(t - 2, ()):
                    if kind in ("xT", "xT2", "xT3"):
                        low_of_norm(kind, u)
                    if kind == "k":
                        low_of_keys(u)
                for kind, b in STATS.get(t - 1, ()):
                    residual_bias(kind, b)
                if t == -27:
                    pool.memset(V[:, :, :, :, HD:], 1.0).then_inc(v_ones, 1)
                    pool.wait_ge(v_ones, 1)
                    pool.wait_ge(resid_ready, 1)
                    set_stack(1)
                    set_stack(2)
                for i, (w, o, lot) in enumerate(PARTS):
                    if t == SPLIT_STEPS[i]:
                        pool.wait_ge(stg_high, i + 1)
                        pool.tensor_tensor(w[1], STG[:, o:o + 512], w[0].bitcast(F32), ALU.subtract).then_inc(stg_low, 1)

        @block.scalar
        def _(act):
            for (v, n), c in zip(vecs, col):
                act.dma_start(ROWV[c:c + n, :], v[0:n * P].rearrange("(r p) -> r p", p=P)).then_inc(vec_in, 16)
            act.dma_start(BV[:, 0, :], b_qkv[2 * D:3 * D].partition_broadcast(P)).then_inc(bvec_in, 16)
            act.dma_start(BV[:, 1, :], b_kv[D:2 * D].partition_broadcast(P)).then_inc(bvec_in, 16)
            for i, v in enumerate((b_ao, b_co, b2)):
                act.dma_start(BO[:, i, :], v.partition_broadcast(P)).then_inc(bvec_in, 16)

            def evacuate(kind, u):
                bank, n = side_slot(kind, u)
                tile = PSD[:, bank, :]
                if kind in ("xT", "xT2", "xT3"):
                    i = norm_index(kind, u)
                    act.wait_ge(side_filled[bank], n + 1)
                    if i:
                        act.wait_ge(xt_low, i)
                    else:
                        act.wait_ge(cols_ready, 1)
                    cs, cb = C_NORM[kind]
                    for c in range(KC):
                        m = act.activation(XT32[:, c, :], tile[:, c * S:(c + 1) * S], ACT.Identity,
                                           scale=COLV[:, cs + c:cs + c + 1], bias=COLV[:, cb + c:cb + c + 1])
                    m.then_inc(xt32_ready, 1)
                if kind == "eT":
                    act.wait_ge(side_filled[bank], n + 1)
                    act.wait_ge(*filled("v", u - 1))
                    act.activation(XS[0][:].rearrange("p c n -> p (c n)"), tile, ACT.Copy).then_inc(e_high, 1)
                if kind == "q":
                    act.wait_ge(side_filled[bank], n + 1)
                    if u:
                        act.wait_ge(q_out, 16 * u)
                    cq = C_Q[u // NB]
                    for c in range(2):
                        m = act.activation(QX[:, 0, c, :], tile[:, c * S:(c + 1) * S], ACT.Identity,
                                           bias=COLV[:, cq + c:cq + c + 1])
                    m.then_inc(q_high, 1)
                if kind == "ctxT":
                    act.wait_ge(side_filled[bank], n + 1)
                    if u:
                        act.wait_ge(*filled("o", u - 1))
                    act.activation(CX[0][:].rearrange("p c n -> p (c n)"), tile, ACT.Copy).then_inc(cx_high, 1)
                if kind == "up":
                    act.wait_ge(side_filled[bank], n + 1)
                    if u >= 2:
                        act.wait_ge(hid_low, u - 1)
                    for c in range(2):
                        k = C_B1 + 2 * (u % 4) + c
                        m = act.activation(G32[:, u % 2, c * S:(c + 1) * S], tile[:, c * S:(c + 1) * S],
                                           ACT.Gelu_apprx_tanh, bias=COLV[:, k:k + 1])
                    m.then_inc(gelu_done, 1)

            def high_of_keys(u):
                act.wait_ge(k32_ready, u + 1)
                if u:
                    act.wait_ge(k_out, 16 * u)
                act.activation(KX[:, 0], K32[:], ACT.Copy).then_inc(k_high, 1)

            flag = act.alloc_register("act_flag")

            def exps(t):
                g, kt, hp, u = t // 4, (t % 4) // 2, t % 2, t // 16
                if t % 16 == 0:
                    act.wait_ge(flags_ready, flags_count(u))
                    act.reg_load(flag, FLG[0:1, mask_of(u):mask_of(u) + 1].bitcast(I32))
                act.wait_ge(b_ready, t + 1)
                with act.If_ne(flag, 0):
                    act.wait_ge(g_fixed[u], t % 16 + 1)
                if t % 4 == 0 and g >= 2:
                    act.wait_ge(pv_done, g - 1)
                if t == 0:
                    act.wait_ge(wqkv_split, 2)
                    act.wait_ge(mask_dif, 2)
                act.activation(PR[:, g % 2, kt, 2 * hp:2 * hp + 2, :],
                               PB[:, t % 2, :].rearrange("p (h n) -> p h n", h=2),
                               ACT.Exp, scale=SCORE_SCALE).then_inc(exp_done, 1)

            def context_out(g):
                act.wait_ge(pv_done, g + 1)
                if g:
                    act.wait_ge(ot_done, g)
                act.activation(O32[:], PV[:, g % 2, 0:S], ACT.Copy).then_inc(o_ready, 1)

            for t in range(FIRST_STEP, LAST_STEP + 1):
                for kind, u in SIDE.get(t - 1, ()):
                    evacuate(kind, u)
                if 0 <= t < CHUNKS:
                    exps(t)
                if t % 4 == 2 and 0 <= (t - 6) // 4 < GROUPS:
                    context_out((t - 6) // 4)
                for kind, u in SIDE.get(t - 2, ()):
                    if kind == "k":
                        high_of_keys(u)
                for i, (w, o, lot) in enumerate(PARTS):
                    if t == SPLIT_STEPS[i]:
                        act.wait_ge(stg_in, 16 * (lot + 2))
                        act.activation(w[0], STG[:, o:o + 512], ACT.Copy).then_inc(stg_high, 1)

        @block.vector
        def _(dve):
            def split_wqkv():
                dve.wait_ge(wqkv_in, 16)
                dve.tensor_copy(WQKV[0][:], RAWQKV).then_inc(wqkv_split, 1)
                dve.wait_ge(wqkv_split, 1)
                dve.tensor_tensor(WQKV[1][:], RAWQKV, WQKV[0][:].bitcast(F32), ALU.subtract).then_inc(wqkv_split, 1)

            def mask_difference(i, lo, hi):
                dve.wait_ge(mask0_in if i == 0 else masks_in, 32)
                dve.tensor_tensor(MK[:, lo:hi], MK[:, lo:hi], MB[:, lo:hi, :].unsqueeze(2).broadcast_to([P, hi - lo, TT, S]),
                                  ALU.not_equal).then_inc(mask_step, 1)
                dve.wait_ge(mask_step, i + 1)
                dve.tensor_reduce(DIF[:, lo:hi], MK[:, lo:hi].rearrange("p j t n -> p j (t n)"), AX.X,
                                  ALU.add).then_inc(mask_dif, 1)

            def mask_flags(i, lo, hi):
                bank, n = side_slot("flags", i)
                dve.wait_ge(side_filled[bank], n + 1)
                k = 5 * i
                dve.tensor_scalar(FLG[:, lo:hi], PSD[:, bank, 0:hi - lo], 1.0, None, ALU.min).then_inc(flag_step, 1)
                dve.wait_ge(flag_step, k + 1)
                dve.tensor_scalar(FLR[:, lo:hi], FLG[:, lo:hi], -1.0, 1.0, ALU.mult, ALU.add).then_inc(flag_step, 1)
                dve.wait_ge(flag_step, k + 2)
                for j in range(lo, hi):
                    m = dve.tensor_scalar(MB[:, j, :], MB[:, j, :], FLR[:, j:j + 1], FLG[:, j:j + 1], ALU.mult, ALU.add)
                m.then_inc(flag_step, 1)
                dve.wait_ge(flag_step, k + 3)
                if i:
                    dve.wait_ge(bias_ready, 1)
                dve.tensor_scalar(BF[:, 0:hi - lo], MB[0:1, lo:hi], -1.0, BIAS, ALU.add, ALU.mult).then_inc(flag_step, 1)
                dve.wait_ge(flag_step, k + 4)
                dve.tensor_copy(BH[i][:, :, 0, :], BF[:, 0:hi - lo]).then_inc(flag_step, 1)
                dve.wait_ge(flag_step, k + 5)
                dve.tensor_tensor(BH[i][:, :, 1, :], BF[:, 0:hi - lo], BH[i][:, :, 0, :].bitcast(F32),
                                  ALU.subtract).then_inc(bias_ready, 1)
                dve.tensor_copy(DIF[:, lo:hi], FLR[:, lo:hi]).then_inc(flags_ready, 1)

            def norm_stats(kind, b):
                n = norm_index(kind, b)
                if kind == "xT":
                    dve.wait_ge(x_in[b], 16)
                else:
                    dve.wait_ge(o_added, b + 1 + (NB if kind == "xT3" else 0))
                for t in range(TT):
                    m = dve.bn_stats(ST[:, n % 2, t, :], X[:, b, t, :])
                m.then_inc(stats_ready, 1)
                dve.wait_ge(stats_ready, n + 1)
                if n >= 2:
                    dve.wait_ge(xn_ready, n - 1)
                for t in range(TT):
                    m = dve.bn_aggr(MV[:, n % 2, t, :], ST[:, n % 2, t, :])
                m.then_inc(mv_ready, 1)

            def normalise(kind, b):
                n = norm_index(kind, b)
                dve.wait_ge(rstd_ready, n + 1)
                if n:
                    dve.wait_ge(*filled(*NORMS[n - 1]))
                for t in range(TT):
                    m = dve.tensor_scalar(XN[:, t, :], X[:, b, t, :], MV[:, n % 2, t, 0:1], RS[:, n % 2, t:t + 1],
                                          ALU.subtract, ALU.mult)
                m.then_inc(xn_ready, 1)

            a_flag = dve.alloc_register("a_flag")
            m_flag = dve.alloc_register("m_flag")
            b_flag = dve.alloc_register("b_flag")

            def evacuate(kind, u):
                bank, n = side_slot(kind, u)
                tile = PSD[:, bank, :]
                if kind in ("cols", "k", "v", "maxT", "o"):
                    dve.wait_ge(side_filled[bank], n + 1)
                if kind == "cols":
                    dve.tensor_copy(COLV[:, 0:NV], tile[:, 0:NV]).then_inc(cols_ready, 1)
                if kind == "flags":
                    mask_flags(u, *((0, 1) if u == 0 else (1, 1 + NB)))
                if kind == "k":
                    if u:
                        dve.wait_ge(k_low, u)
                    else:
                        dve.wait_ge(cols_ready, 1)
                    if u in (0, NB):
                        dve.wait_ge(flag_step, 5 * (u // NB) + 3)
                    ck = C_K[u // NB]
                    for c in range(2):
                        m = dve.scalar_tensor_tensor(K32[:, c, :], tile[:, c * S:(c + 1) * S], COLV[:, ck + c:ck + c + 1],
                                                     MB[:, mask_of(u), :], ALU.add, ALU.mult)
                    m.then_inc(k32_ready, 1)
                if kind == "v":
                    if u == 0:
                        dve.wait_ge(bvec_in, 16 * 5)
                    if u >= 2:
                        dve.wait_ge(pv_done, 4 * (u - 1))
                    dve.tensor_tensor(V[:, u % 2, :, :, 0:HD], tile.rearrange("p (t h d) -> p t h d", t=TT, h=NH),
                                      BV[:, u // NB, :].rearrange("p (h d) -> p h d", h=NH).unsqueeze(1)
                                      .broadcast_to([P, TT, NH, HD]), ALU.add).then_inc(v_ready, 1)
                if kind == "maxT":
                    s, j = u, mask_of(u // 2)
                    dve.reg_load(m_flag, FLG[0:1, j:j + 1].bitcast(I32))
                    with dve.If_ne(m_flag, 0):
                        if s % 2:
                            dve.wait_ge(g_max_out[s // 2], 16)
                        dve.tensor_scalar(CG[:], tile[0:HH, 0:S], -1.0, None, ALU.mult).then_inc(g_max_ready[s // 2], 1)
                    if s >= 2:
                        dve.wait_ge(crow_in, 16 * (s - 1))
                    dve.tensor_scalar(CR[:, s % 2, :], tile[0:HH, 0:S], FLR[0:HH, j:j + 1], -1.0, ALU.mult,
                                      ALU.mult).then_inc(crow_ready, 1)
                if kind == "o":
                    b = u % NB
                    dve.wait_ge(resid_ready, norm_index("xT" if u < NB else "xT2", b) + 1)
                    xb = X[:, b].rearrange("p t d -> p (t d)")
                    dve.tensor_tensor(xb, xb, tile, ALU.add).then_inc(o_added, 1)

            def split(kind, u):
                bank, n = side_slot(kind, u)
                tile = PSD[:, bank, :]
                if kind in ("xT", "xT2", "xT3"):
                    dve.wait_ge(xt32_ready, norm_index(kind, u) + 1)
                    if norm_dst_used(kind, u):
                        dve.wait_ge(*filled(*norm_dst_used(kind, u)))
                    dve.tensor_copy(norm_dst(kind, u)[0][:], XT32[:]).then_inc(xt_high, 1)
                if kind == "eT":
                    dve.wait_ge(e_high, u - NB + 1)
                    dve.tensor_tensor(XS[1][:].rearrange("p c n -> p (c n)"), tile,
                                      XS[0][:].bitcast(F32).rearrange("p c n -> p (c n)"), ALU.subtract).then_inc(e_low, 1)
                if kind == "q":
                    dve.wait_ge(q_high, u + 1)
                    cq = C_Q[u // NB]
                    for c in range(2):
                        m = dve.scalar_tensor_tensor(QX[:, 1, c, :], tile[:, c * S:(c + 1) * S], COLV[:, cq + c:cq + c + 1],
                                                     QX[:, 0, c, :].bitcast(F32), ALU.add, ALU.subtract)
                    m.then_inc(q_low, 1)
                if kind == "ctxT":
                    dve.wait_ge(cx_high, u + 1)
                    dve.tensor_tensor(CX[1][:].rearrange("p c n -> p (c n)"), tile,
                                      CX[0][:].bitcast(F32).rearrange("p c n -> p (c n)"), ALU.subtract).then_inc(cx_low, 1)
                if kind == "up":
                    m_ = u
                    c2 = 2 * (m_ % 4)
                    dve.wait_ge(gelu_done, m_ + 1)
                    if m_ >= 4:
                        dve.wait_ge(down_done, m_ - 3)
                    else:
                        dve.wait_ge(b_ready, CHUNKS)
                    g = G32[:, m_ % 2, :].rearrange("p (c n) -> p c n", c=2)
                    dve.tensor_copy(HID[0][:, c2:c2 + 2, :], g).then_inc(hid_high, 1)
                    dve.wait_ge(hid_high, m_ + 1)
                    dve.tensor_tensor(HID[1][:, c2:c2 + 2, :], g, HID[0][:, c2:c2 + 2, :].bitcast(F32),
                                      ALU.subtract).then_inc(hid_low, 1)

            def maxima(a):
                s, i, u = a // 8, a % 8, a // 16
                qt, hp = i // 4, i % 4
                j, k = mask_of(u), 3 * (a % 16)
                if a % 16 == 0:
                    dve.wait_ge(flags_ready, flags_count(u))
                    dve.reg_load(a_flag, FLG[0:1, j:j + 1].bitcast(I32))
                dve.wait_ge(a_ready, a + 1)
                tile = PA[:, a % 2, :].rearrange("p (h n) -> p h n", h=2)
                with dve.If_ne(a_flag, 0):
                    if a % 16 == 0:
                        dve.wait_ge(g_mask_in[u], 16)
                    dve.tensor_scalar(MBI[:, 0, :], MG[:, qt, :], -1.0, BIAS, ALU.add, ALU.mult).then_inc(g_step_a[u], 1)
                    dve.tensor_tensor(tile, tile, MG[:, qt, :].unsqueeze(1).broadcast_to([P, 2, S]),
                                      ALU.mult).then_inc(g_step_a[u], 1)
                    dve.wait_ge(g_step_a[u], k + 2)
                    dve.tensor_tensor(tile, tile, MBI[:, 0, :].unsqueeze(1).broadcast_to([P, 2, S]),
                                      ALU.add).then_inc(g_step_a[u], 1)
                    dve.wait_ge(g_step_a[u], k + 3)
                if i == 0 and s >= 2:
                    dve.wait_ge(*filled("maxT", s - 2))
                dve.tensor_reduce(MX[:, s % 2, qt, 2 * hp:2 * hp + 2], tile, AX.X, ALU.max).then_inc(max_done, 1)

            def mask_scores(t):
                s, i, u = t // 8, t % 8, t // 16
                kt, h0 = (i % 4) // 2, 4 * (i // 4) + 2 * (i % 2)
                j, k = mask_of(u), 3 * (t % 16)
                if t % 16 == 0:
                    dve.reg_load(b_flag, FLG[0:1, j:j + 1].bitcast(I32))
                with dve.If_ne(b_flag, 0):
                    dve.wait_ge(b_ready, t + 1)
                    if i == 0:
                        dve.wait_ge(g_mask_in[u], 16 * (1 + TT))
                        dve.wait_ge(g_bcast_in[u], 16 * (s % 2 + 1))
                    tile = PB[:, t % 2, :].rearrange("p (h n) -> p h n", h=2)
                    dve.tensor_scalar(MBI[:, 1, :], MGT[:, kt, :], -1.0, BIAS, ALU.add, ALU.mult).then_inc(g_step_b[u], 1)
                    dve.tensor_tensor(tile, tile, MGT[:, kt, :].unsqueeze(1).broadcast_to([P, 2, S]),
                                      ALU.mult).then_inc(g_step_b[u], 1)
                    dve.wait_ge(g_step_b[u], k + 2)
                    dve.tensor_tensor(tile, tile, MBI[:, 1, :].unsqueeze(1).broadcast_to([P, 2, S]),
                                      ALU.add).then_inc(g_step_b[u], 1)
                    dve.wait_ge(g_step_b[u], k + 3)
                    dve.tensor_tensor(tile, tile, CB[:, h0:h0 + 2, :], ALU.add).then_inc(g_fixed[u], 1)
                    dve.wait_ge(g_fixed[u], t % 16 + 1)

            def normalise_context(g):
                u, r = g // 4, g % 2
                dve.wait_ge(ot_done, g + 1)
                src = PV[:, r, S:2 * S].rearrange("p (th w) -> p th w", w=2 * HD)
                dve.reciprocal(RC[:, r, :], src[:, :, HD]).then_inc(recip_done, 1)
                dve.wait_ge(recip_done, g + 1)
                if g % 4 == 0 and u:
                    dve.wait_ge(*filled("ctxT", u - 1))
                h = (g % 4) * 4 * HD
                dve.tensor_tensor(CT[:, :, h:h + 4 * HD].rearrange("p t (h d) -> p t h d", h=4),
                                  src.rearrange("p (t h) w -> p t h w", t=TT)[:, :, :, 0:HD],
                                  RC[:, r, :].rearrange("p (t h) -> p t h", t=TT).unsqueeze(3)
                                  .broadcast_to([P, TT, 4, HD]), ALU.mult).then_inc(ctx_done, 1)

            def finish(b):
                acc = (PA, PB)[b % 2]
                dve.wait_ge(down_done, 4 * b + 4)
                dve.wait_ge(resid_ready, norm_index("xT3", b) + 1)
                dve.tensor_tensor(X[:, b], X[:, b], acc[:, :, 0:D], ALU.add).then_inc(fin_done, 1)

            for t in range(FIRST_STEP, LAST_STEP + 1):
                for kind, u in SIDE.get(t - 1, ()):
                    evacuate(kind, u)
                if 0 <= t + LEAD < CHUNKS:
                    maxima(t + LEAD)
                if 0 <= t < CHUNKS:
                    mask_scores(t)
                for kind, u in SIDE.get(t - 2, ()):
                    split(kind, u)
                if t % 4 == 0 and 0 <= t // 4 - 2 < GROUPS:
                    normalise_context(t // 4 - 2)
                for kind, b in STATS.get(t - 1, ()):
                    normalise(kind, b)
                for kind, b in STATS.get(t, ()):
                    norm_stats(kind, b)
                if t == -31:
                    split_wqkv()
                    mask_difference(0, 0, 1)
                if t == -18:
                    mask_difference(1, 1, 1 + NB)
                if t in FINISH:
                    finish(FINISH[t])

        @block.tensor
        def _(pe):
            def three(dst, lhs, rhs, first, last):
                pe.matmul(dst, lhs[0], rhs[0], start=first, stop=False)
                pe.matmul(dst, lhs[0], rhs[1], start=False, stop=False)
                return pe.matmul(dst, lhs[1], rhs[0], start=False, stop=last)

            def project_cols(tile, w, lo, src):
                for c in range(2):
                    for k in range(KC):
                        o = lo + c * P
                        m = three(tile[:, c * S:(c + 1) * S], [t[:, k, o:o + P] for t in w], [t[:, k, :] for t in src],
                                  k == 0, k == KC - 1)
                return m

            def project_rows(tile, src, w, lo):
                for t in range(TT):
                    for k in range(KC):
                        m = three(tile[:, t * D:(t + 1) * D], [s[:, k, t * P:(t + 1) * P] for s in src],
                                  [v[:, k, lo:lo + D] for v in w], k == 0, k == KC - 1)
                return m

            def transpose_rows(tile, src):
                for k in range(KC):
                    for t in range(TT):
                        o = k * S + t * P
                        m = pe.transpose(tile[:, o:o + P], src[:, t, k * P:(k + 1) * P], IDN[:])
                return m

            def side(kind, u):
                bank, n = side_slot(kind, u)
                tile = PSD[:, bank, :]
                j = SIDE_ORDER.index((kind, u))
                if j >= 2:
                    pe.wait_ge(*drained(*SIDE_ORDER[j - 2]))
                if kind == "cols":
                    pe.wait_ge(const_ready, 3)
                    pe.wait_ge(vec_in, 16 * len(vecs))
                    m = pe.transpose(tile[:, 0:NV], ROWV[0:NV, :], IDN[0:NV, 0:NV])
                elif kind == "flags":
                    lo, hi = (0, 1) if u == 0 else (1, 1 + NB)
                    pe.wait_ge(mask_dif, u + 1)
                    m = pe.matmul(tile[:, 0:hi - lo], ONE, DIF[:, lo:hi], start=True, stop=True)
                elif kind in ("xT", "xT2", "xT3"):
                    pe.wait_ge(xn_ready, norm_index(kind, u) + 1)
                    m = transpose_rows(tile, XN)
                elif kind == "eT":
                    pe.wait_ge(e_in, 16 * (u - NB + 1))
                    m = transpose_rows(tile, E)
                elif kind == "q":
                    if u < NB:
                        pe.wait_ge(xt_low, norm_index("xT", u) + 1)
                        if u == 0:
                            pe.wait_ge(wqkv_split, 2)
                        m = project_cols(tile, WQKV, 0, XS)
                    else:
                        pe.wait_ge(xt_low, norm_index("xT2", u - NB) + 1)
                        pe.wait_ge(stg_low, W_QUERY_DONE)
                        m = project_cols(tile, WQ, 0, XC)
                elif kind == "k":
                    if u < NB:
                        m = project_cols(tile, WQKV, D, XS)
                    else:
                        pe.wait_ge(e_low, u - NB + 1)
                        pe.wait_ge(stg_low, W_KV_DONE)
                        m = project_cols(tile, WKV, 0, XS)
                elif kind == "v":
                    m = project_rows(tile, XS, WQKV if u < NB else WKV, 2 * D if u < NB else D)
                elif kind == "maxT":
                    pe.wait_ge(max_done, 8 * u + 8)
                    for t in range(TT):
                        m = pe.transpose(tile[0:HH, t * P:(t + 1) * P], MX[:, u % 2, t, :], IDN[:])
                elif kind == "ctxT":
                    pe.wait_ge(ctx_done, 4 * u + 4)
                    m = transpose_rows(tile, CT)
                elif kind == "o":
                    pe.wait_ge(cx_low, u + 1)
                    pe.wait_ge(stg_low, W_AO_DONE if u < NB else W_CO_DONE)
                    m = project_rows(tile, CX, WAO if u < NB else WCO, 0)
                elif kind == "up":
                    b = u // 4
                    if u % 4 == 0:
                        pe.wait_ge(xt_low, norm_index("xT3", b) + 1)
                        pe.wait_ge(stg_low, W_MLP_DONE)
                    m = project_cols(tile, W1, 2 * P * (u % 4), norm_dst("xT3", b))
                m.then_inc(side_filled[bank], 1)

            def scores_for_maxima(a):
                s, i = a // 8, a % 8
                r, qt, hp = s % RING, i // 4, i % 4
                if i == 0:
                    pe.wait_ge(stacked[r], stack_count(s))
                if a >= 2:
                    pe.wait_ge(max_done, a - 1)
                for n in range(2):
                    h = 2 * hp + n
                    m = pe.matmul(PA[:, a % 2, n * S:(n + 1) * S], QS[0:ROWS_A, r, h, qt * P:(qt + 1) * P],
                                  KS[0:ROWS_A, r, h, :], start=True, stop=True)
                m.then_inc(a_ready, 1)

            def scores_for_exp(t):
                s, i = t // 8, t % 8
                r, kt, h0 = s % RING, (i % 4) // 2, 4 * (i // 4) + 2 * (i % 2)
                if i == 0:
                    pe.wait_ge(crow_in, 16 * (s + 1))
                if t >= 2:
                    pe.wait_ge(exp_done, t - 1)
                for n in range(2):
                    m = pe.matmul(PB[:, t % 2, n * S:(n + 1) * S], KS[0:ROWS_B, r, h0 + n, kt * P:(kt + 1) * P],
                                  QS[0:ROWS_B, r, h0 + n, :], start=True, stop=True)
                m.then_inc(b_ready, 1)

            def context(g):
                u, r = g // 4, g % 2
                pe.wait_ge(exp_done, 4 * g + 4)
                if g % 4 == 0:
                    pe.wait_ge(v_ready, u + 1)
                    pe.wait_ge(v_ones, 1)
                if g >= 2:
                    pe.wait_ge(ctx_done, g - 1)
                for kt in range(TT):
                    for n in range(4):
                        m = pe.matmul(PV[32 * n:32 * n + 32, r, 0:S], V[:, u % 2, kt, 4 * (g % 4) + n, :],
                                      PR[:, r, kt, n, :], start=(kt == 0), stop=(kt == TT - 1),
                                      tile_position=(0, 32 * n))
                m.then_inc(pv_done, 1)

            def transpose_context(g):
                r = g % 2
                pe.wait_ge(o_ready, g + 1)
                for t in range(TT):
                    m = pe.transpose(PV[:, r, S + t * P:S + (t + 1) * P], O32[:, t * P:(t + 1) * P], IDN[:])
                m.then_inc(ot_done, 1)

            def down(m_):
                b, c = m_ // 4, m_ % 4
                acc = (PA, PB)[b % 2]
                pe.wait_ge(hid_low, m_ + 1)
                if c == 0:
                    if b < 2:
                        pe.wait_ge(*((max_done, CHUNKS), (exp_done, CHUNKS))[b])
                    else:
                        pe.wait_ge(fin_done, b - 1)
                for t in range(TT):
                    for k in (2 * c, 2 * c + 1):
                        m = three(acc[:, t, 0:D], [h[:, k, t * P:(t + 1) * P] for h in HID], [w[:, k, :] for w in W2],
                                  k == 0, k == FC - 1)
                m.then_inc(down_done, 1)

            for t in range(FIRST_STEP, LAST_STEP + 1):
                if 0 <= t + LEAD < CHUNKS:
                    scores_for_maxima(t + LEAD)
                if 0 <= t < CHUNKS:
                    scores_for_exp(t)
                if t % 4 == 1 and 0 <= (t - 5) // 4 < GROUPS:
                    context((t - 5) // 4)
                if t % 4 == 3 and 0 <= (t - 7) // 4 < GROUPS:
                    transpose_context((t - 7) // 4)
                for kind, u in SIDE.get(t, ()):
                    side(kind, u)
                if t in DOWN:
                    down(DOWN[t])


_INS = ["x", "ctx_2048", "mask_1x1xSxS2_fc1", "mask_Bx1xSxS2_ff1"] + ["L0_xattn_" + n for n in (
    "ln1_s", "ln1_b", "w_qkv", "b_qkv", "w_ao", "b_ao", "ln2_s", "ln2_b", "w_q", "b_q", "w_kv", "b_kv",
    "w_co", "b_co", "ln3_s", "ln3_b", "w1", "b1", "w2", "b2")]


def kernel(**inputs):
    import numpy as _np
    import concourse.bacc as _bacc
    from concourse import mybir as _mybir
    from concourse.bass_utils import run_bass_kernel_spmd as _run

    nc = _bacc.Bacc("TRN2", target_bir_lowering=False, num_devices=1)
    arrays, args = {}, []
    for name in _INS:
        a = _np.ascontiguousarray(inputs[name])
        arrays[f"in_{name}_dram"] = a
        args.append(nc.dram_tensor(f"in_{name}_dram", a.shape, _mybir.dt.from_np(a.dtype), kind="ExternalInput").ap())
    args.append(nc.dram_tensor("out_0_dram", (NB, S, D), _mybir.dt.float32, kind="ExternalOutput").ap())
    decoder_layer(nc, *args)
    r = _run(nc, [arrays], core_ids=[0])
    return r.results[0]["out_0_dram"]
```

```python
from contextlib import ExitStack

import concourse.bass as bass
from concourse import mybir

F32 = mybir.dt.float32
F32R = mybir.dt.float32r
I32 = mybir.dt.int32
ALU = mybir.AluOpType
ACT = mybir.ActivationFunctionType
AX = mybir.AxisListType

NB, S, D, NH = 4, 256, 256, 16
HD = D // NH
FF = 4 * D
P = 128
TT = S // P
KC = D // P
FC = FF // P
EPS = 1e-5
SCORE_SCALE = HD ** -0.5
BIAS = 10000.0 * HD ** 0.5
UNITS = 2 * NB
HALVES = 2 * UNITS
HH = NH // 2
CHUNKS = 8 * HALVES
GROUPS = 4 * UNITS
LEAD = 13
RING = 4
ROWS_A, ROWS_B, CROW = 50, 51, 50
XT3_STEPS = (101, 117, 132, 142)
PIECES = NB * FC // 2
UP_STEPS = (106, 112, 114, 119, 123, 125, 129, 131, 136, 137, 139, 140, 146, 147, 148, 149)
GELU_STEPS = (128, 129, 130, 130, 131, 131, 132, 133, 137, 138, 140, 141, 147, 148, 149, 150)
DOWN_STEPS = (130, 131, 132, 133, 134, 135, 136, 137, 141, 142, 143, 144, 149, 150, 151, 152)
EARLY = 8


def side_plan():
    plan = {}

    def put(t, kind, u):
        plan.setdefault(t, []).append((kind, u))

    put(-33, "cols", 0)
    put(-28, "flags", 0)
    put(-18, "flags", 1)
    for u in range(UNITS):
        t = 16 * u
        if u < NB:
            put(t - 30, "xT", u)
            put(t + 37, "xT2", u)
        else:
            put(t - 30, "eT", u)
        put(t - 25, "k", u)
        put(t - 22, "q", u)
        put(t - 16, "v", u)
        put(t - 4, "maxT", 2 * u)
        put(t + 4, "maxT", 2 * u + 1)
        put({6: 121, 7: 134}.get(u, t + 24), "ctxT", u)
        put({6: 127, 7: 138}.get(u, t + 30), "o", u)
    for b, t in enumerate(XT3_STEPS):
        put(t, "xT3", b)
    for m in range(PIECES):
        put(UP_STEPS[m], "up", m)
    return plan



SIDE = side_plan()
FIRST_STEP = -35
LAST_STEP = DOWN_STEPS[-1] + 1
LOT = 1024
HALVED = ("k", "q", "v", "o", "up")
SIDE_ORDER = [x for t in sorted(SIDE) for x in SIDE[t]]
NORMS = [x for x in SIDE_ORDER if x[0] in ("xT", "xT2", "xT3")]


def stats_step(kind, b):
    return {"xT": 16 * b - 34, "xT2": 16 * b + 31, "xT3": (95, 111, 128, 139)[b % NB]}[kind]


STATS = {}
for _kind, _b in NORMS:
    STATS.setdefault(stats_step(_kind, _b), []).append((_kind, _b))


def side_slot(kind, u):
    j = SIDE_ORDER.index((kind, u))
    return j % 2, j // 2


def norm_index(kind, b):
    return NORMS.index((kind, b))


def decoder_layer(nc, x, ctx_in, self_mask, cross_mask, ln1_s, ln1_b, w_qkv, b_qkv, w_ao, b_ao,
                  ln2_s, ln2_b, w_q, b_q, w_kv, b_kv, w_co, b_co, ln3_s, ln3_b, w1, b1, w2, b2, out):
    with ExitStack() as stack:
        def sb(name, shape, dt=F32):
            return stack.enter_context(nc.sbuf_tensor(name, shape, dt))

        def ps(name, shape):
            return stack.enter_context(nc.psum_tensor(name, shape, F32))

        def sem(name):
            return stack.enter_context(nc.semaphore(name))

        def dram(name, shape):
            return nc.dram_tensor(name, shape, F32, kind="Internal").ap()

        q_scr = dram("q_scr", (UNITS, NH, HD, 3, S))
        k_scr = dram("k_scr", (UNITS, NH, HD, 3, S))
        bias_scr = dram("bias_scr", (1 + NB, 2, S))
        max_scr = dram("max_scr", (HALVES, HH, S))

        X = sb("X", [P, NB, TT, D])
        E = sb("E", [P, TT, D])
        WQKV = [sb(f"WQKV{i}", [P, KC, 3 * D], F32R) for i in range(2)]
        WAO = [sb(f"WAO{i}", [P, KC, D], F32R) for i in range(2)]
        WQ = [sb(f"WQ{i}", [P, KC, D], F32R) for i in range(2)]
        WKV = [sb(f"WKV{i}", [P, KC, 2 * D], F32R) for i in range(2)]
        WCO = [sb(f"WCO{i}", [P, KC, D], F32R) for i in range(2)]
        W1 = [sb(f"W1{i}", [P, KC, FF], F32R) for i in range(2)]
        W2 = [sb(f"W2{i}", [P, FC, D], F32R) for i in range(2)]
        QS = sb("QS", [P, 2, HH, S], F32R)
        KS = sb("KS", [P, 2, HH, S], F32R)
        PRE = sb("PRE", [P, EARLY, 2, S], F32R)
        HID = [[t[:, b] for t in (KS, QS)] for b in range(2)]
        PR = sb("PR", [P, 2, 2, 4, S])
        RAW = PR[:].rearrange("p a b c n -> p (a b c n)")
        RAWQKV = RAW[:, 0:KC * 3 * D].rearrange("p (c n) -> p c n", c=KC)
        MK = RAW[:, KC * 3 * D:4096].rearrange("p (j t n) -> p j t n", j=1 + NB, t=TT)
        STG = sb("STG", [P, LOT])
        CB = sb("CB", [P, HH, S])
        V = sb("V", [P, 2, TT, NH, 2 * HD])
        XN = sb("XN", [P, TT, D])
        XT32 = sb("XT32", [P, KC, S])
        XS = [sb(f"XS{i}", [P, KC, S], F32R) for i in range(2)]
        XC = [sb(f"XC{i}", [P, KC, S], F32R) for i in range(2)]
        QX = sb("QX", [P, 2, 2, S], F32R)
        KX = sb("KX", [P, 2, 2, S], F32R)
        K32 = sb("K32", [P, 2, S])
        O32 = sb("O32", [P, S])
        RC = sb("RC", [P, 2, TT * 4])
        CT = sb("CT", [P, TT, D])
        CX = [sb(f"CX{i}", [P, KC, S], F32R) for i in range(2)]
        G32 = STG[:].rearrange("p (a n) -> p a n", a=2)
        MBI = sb("MBI", [P, 2, S])
        BF = CB[0:1, 4:8, :]
        BH = [PRE[0:1, 0:1], PRE[0:1, 1:1 + NB]]
        MB = sb("MB", [P, 1 + NB, S])
        MG = sb("MG", [P, TT, S])
        MGT = sb("MGT", [P, TT, S])
        DIF = sb("DIF", [P, 1 + NB])
        FLG = sb("FLG", [P, 1 + NB])
        FLR = sb("FLR", [P, 1 + NB])
        NFR = sb("NFR", [P, 1 + NB])
        MX = sb("MX", [P, 2, TT, HH])
        CR = sb("CR", [HH, 2, S], F32R)
        CG = sb("CG", [HH, S])
        ROWV = CB[0:32, 0, 0:P]
        COLV = sb("COLV", [P, 32])
        BO = sb("BO", [P, 3, D])
        IDN = sb("IDN", [P, P])
        ONE = CB[:, 1, 0:P]
        ST = sb("ST", [P, 2, TT, 6])
        MV = sb("MV", [P, 2, TT, 2])
        RS = sb("RS", [P, 2, TT])
        NEGH = sb("NEGH", [P, TT])

        vecs = [(ln1_s, 2), (ln1_b, 2), (b_qkv, 6), (ln2_s, 2), (ln2_b, 2), (b_q, 2), (b_kv, 4),
                (ln3_s, 2), (ln3_b, 2), (b1, 8)]
        col = [sum(n for _, n in vecs[:i]) for i in range(len(vecs))]
        NV = sum(n for _, n in vecs)
        C_NORM = {"xT": (col[0], col[1]), "xT2": (col[3], col[4]), "xT3": (col[7], col[8])}
        C_Q, C_K, C_V, C_B1 = (col[2], col[5]), (col[2] + 2, col[6]), (col[2] + 4, col[6] + 2), col[9]

        PA = ps("PA", [P, 2, 512])
        PB = ps("PB", [P, 2, 512])
        PV = ps("PV", [P, 2, 512])
        PSD = ps("PSD", [P, 2, 512])

        MLP_OUT = (PA, PB, PA, PB)

        x_in = [sem(f"x_in{b}") for b in range(NB)]
        e_in, vec_in, bvec_in = sem("e_in"), sem("vec_in"), sem("bvec_in")
        wqkv_in, mask0_in, masks_in, stg_in = sem("wqkv_in"), sem("mask0_in"), sem("masks_in"), sem("stg_in")
        stg_high, stg_low, wqkv_split = sem("stg_high"), sem("stg_low"), sem("wqkv_split")
        id_zero, const_ready, stack_set, v_ones = sem("id_zero"), sem("const_ready"), sem("stack_set"), sem("v_ones")
        cols_ready, flags_ready, bias_ready = sem("cols_ready"), sem("flags_ready"), sem("bias_ready")
        bias_out, mask_step, mask_dif, flag_step = sem("bias_out"), sem("mask_step"), sem("mask_dif"), sem("flag_step")
        stats_ready, mv_ready = sem("stats_ready"), sem("mv_ready")
        rstd_step, rstd_ready = sem("rstd_step"), sem("rstd_ready")
        xn_ready, resid_ready = sem("xn_ready"), sem("resid_ready")
        xt32_ready, xt_high, xt_low = sem("xt32_ready"), sem("xt_high"), sem("xt_low")
        e_high, e_low, q_high, q_low = sem("e_high"), sem("e_low"), sem("q_high"), sem("q_low")
        k32_ready, k_high, k_low, v_ready = sem("k32_ready"), sem("k_high"), sem("k_low"), sem("v_ready")
        q_out, k_out = sem("q_out"), sem("k_out")
        stacked = [sem(f"stacked{r}") for r in range(RING)]
        side_filled = [sem(f"side_filled{i}") for i in range(2)]
        a_ready, max_done, crow_ready, crow_in = sem("a_ready"), sem("max_done"), sem("crow_ready"), sem("crow_in")
        b_ready, exp_done, pv_done, o_ready = sem("b_ready"), sem("exp_done"), sem("pv_done"), sem("o_ready")
        ot_done, recip_done, ctx_done = sem("ot_done"), sem("recip_done"), sem("ctx_done")
        cx_high, cx_low, o_added = sem("cx_high"), sem("cx_low"), sem("o_added")
        pre_ready = sem("pre_ready")
        gelu_done, hid_high, hid_low, down_done = sem("gelu_done"), sem("hid_high"), sem("hid_low"), sem("down_done")
        fin_done, out_done = sem("fin_done"), sem("out_done")
        g_mask_in = [sem(f"g_mask_in{u}") for u in range(UNITS)]
        g_max_ready = [sem(f"g_max_ready{u}") for u in range(UNITS)]
        g_max_out = [sem(f"g_max_out{u}") for u in range(UNITS)]
        g_bcast_in = [sem(f"g_bcast_in{u}") for u in range(UNITS)]
        g_fixed = [sem(f"g_fixed{u}") for u in range(UNITS)]
        g_step_a = [sem(f"g_step_a{u}") for u in range(UNITS)]
        g_step_b = [sem(f"g_step_b{u}") for u in range(UNITS)]

        def mask_of(u):
            return 0 if u < NB else 1 + u - NB

        def mask_dram(j):
            return self_mask[0, 0] if j == 0 else cross_mask[j - 1, 0]

        def flags_count(u):
            return 1 if u < NB else 2

        def stack_rows(t, s, lo, hi):
            first = 64 * (s // 2 % 2)
            return t[first + lo:first + hi, s % 2]

        def stack_dmas(s):
            return 3 if s < RING or s >= 2 * NB else 2

        def stack_count(s):
            return 16 * sum(stack_dmas(i) for i in range(s % RING, s + 1, RING))

        def filled(kind, u):
            bank, n = side_slot(kind, u)
            return side_filled[bank], n + 1

        def drained(kind, u):
            return {
                "cols": lambda: (cols_ready, 1),
                "flags": lambda: (flag_step, 5 * u + 1),
                "xT": lambda: (xt32_ready, norm_index(kind, u) + 1),
                "xT2": lambda: (xt32_ready, norm_index(kind, u) + 1),
                "xT3": lambda: (xt32_ready, norm_index(kind, u) + 1),
                "eT": lambda: (e_low, u - NB + 1),
                "q": lambda: (q_low, u + 1),
                "k": lambda: (k32_ready, u + 1),
                "v": lambda: (v_ready, u + 1),
                "maxT": lambda: (crow_ready, u + 1),
                "ctxT": lambda: (cx_low, u + 1),
                "o": lambda: (o_added, u + 1),
                "up": lambda: (pre_ready if u < EARLY else gelu_done, u + 1),
            }[kind]()

        def norm_dst(kind, b):
            if kind == "xT":
                return XS
            if kind == "xT2":
                return XC
            return (XS, XC)[b % 2]

        def norm_dst_used(kind, b):
            if kind == "xT":
                return ("v", b - 1) if b else None
            if kind == "xT2":
                return ("q", NB + b - 1) if b else None
            return (("v", UNITS - 1), ("q", UNITS - 1), ("up", 3), ("up", 7))[b]

        def flat(w, lo, hi):
            return [t[:].rearrange("p c n -> p (c n)")[:, lo:hi] for t in w]

        PARTS = []
        for lot, pieces in enumerate(([(WAO, 0, 512), (WQ, 0, 512)], [(WKV, 0, 1024)], [(W1, 0, 1024)],
                                      [(W1, 1024, 2048)], [(W2, 0, 1024)], [(W2, 1024, 2048)], [(WCO, 0, 512)])):
            o = 0
            for w, lo, hi in pieces:
                for c in range(lo, hi, 512):
                    PARTS.append((flat(w, c, c + 512), o, lot))
                    o += 512
        SPLIT_STEPS = [-12, -11, 0, 1, 14, 15, 28, 31, 44, 45, 60, 61, 76]

        def parts_before(lot):
            return sum(1 for p in PARTS if p[2] < lot)

        W_AO_DONE, W_QUERY_DONE, W_KV_DONE, W_MLP_DONE, W_CO_DONE = 1, 2, 4, 12, 13

        block = stack.enter_context(nc.Block())

        @block.sync
        def _(sp):
            def load(dst, src, s):
                sp.dma_start(dst, src).then_inc(s, 16)

            def rows(ap):
                return ap.rearrange("(c p) n -> p c n", p=P)

            def load_lot(lot):
                if lot:
                    sp.wait_ge(stg_low, parts_before(lot))
                halves = [STG[:, 0:512].rearrange("p (c n) -> p c n", c=KC),
                          STG[:, 512:1024].rearrange("p (c n) -> p c n", c=KC)]
                if lot == 0:
                    load(halves[0], rows(w_ao), stg_in)
                    load(halves[1], rows(w_q), stg_in)
                elif lot == 1:
                    load(STG[:].rearrange("p (c n) -> p c n", c=KC), rows(w_kv), stg_in)
                elif lot in (2, 3):
                    load(STG[:], w1[(lot - 2) * P:(lot - 1) * P, :], stg_in)
                elif lot in (4, 5):
                    load(STG[:].rearrange("p (c n) -> p c n", c=4), rows(w2[(lot - 4) * 4 * P:(lot - 3) * 4 * P, :]), stg_in)
                else:
                    load(halves[0], rows(w_co), stg_in)

            load(X[:, 0], x[0].rearrange("(t p) d -> p t d", p=P), x_in[0])
            load(RAWQKV, rows(w_qkv), wqkv_in)
            load(MB[:, 0, :], self_mask[0, 0, 0, :].partition_broadcast(P), mask0_in)
            load(MK[:, 0], self_mask[0, 0].rearrange("(t p) n -> p t n", p=P), mask0_in)
            sp.wait_ge(vec_in, 16 * len(vecs))
            load(X[:, 1], x[1].rearrange("(t p) d -> p t d", p=P), x_in[1])
            load_lot(0)
            load(MB[:, 1:], cross_mask[:, 0, 0, :].partition_broadcast(P), masks_in)
            load(MK[:, 1:], cross_mask[:, 0].rearrange("b (t p) n -> p (b t) n", p=P).rearrange(
                "p (b t) n -> p b t n", t=TT), masks_in)
            for b in (2, 3):
                load(X[:, b], x[b].rearrange("(t p) d -> p t d", p=P), x_in[b])
            load(E[:], ctx_in[0].rearrange("(t p) d -> p t d", p=P), e_in)
            sp.wait_ge(bias_ready, 1)
            load(bias_scr[0:1], BH[0].bitcast(F32), bias_out)

            def write_split(u, split, scr, high, low, out, parts):
                for part, l in sorted(enumerate(parts), key=lambda x: x[1]):
                    sp.wait_ge((high, low)[l], u + 1)
                    load(scr[u, :, :, part].rearrange("(t h) d n -> (h d) t n", t=2), split[:, l].bitcast(F32), out)

            def load_stack(s):
                u, r, h0 = s // 2, s % RING, HH * (s % 2)
                if s < RING:
                    sp.wait_ge(stack_set, 2 * (s // 2 + 1))
                else:
                    sp.wait_ge(b_ready, 8 * (s - RING + 1))
                for dst, scr, s_out in ((KS, k_scr, k_out), (QS, q_scr, q_out)):
                    sp.wait_ge(s_out, 48 * (u + 1))
                    load(stack_rows(dst, s, 0, 3 * HD).bitcast(F32),
                         scr[u, h0:h0 + HH].rearrange("h d l n -> (d l) h n"), stacked[r])
                if stack_dmas(s) == 3:
                    j = mask_of(u)
                    sp.wait_ge(bias_out, 16 if j == 0 else 32)
                    load(stack_rows(KS, s, 3 * HD, 3 * HD + 2).bitcast(F32),
                         bias_scr[j].unsqueeze(1).broadcast_to([2, HH, S]), stacked[r])

            flag = sp.alloc_register("sp_flag")

            def masks_by_query(u):
                j = mask_of(u)
                sp.wait_ge(flags_ready, flags_count(u))
                sp.reg_load(flag, FLG[0:1, j:j + 1].bitcast(I32))
                with sp.If_ne(flag, 0):
                    if u:
                        sp.wait_ge(max_done, 16 * u)
                    load(MG[:], mask_dram(j).rearrange("(t p) n -> p t n", p=P), g_mask_in[u])

            for t in range(FIRST_STEP, CHUNKS):
                u = (t + 22) // 16
                if 0 <= u < UNITS:
                    if t == 16 * u - 22:
                        write_split(u, KX, k_scr, k_high, k_low, k_out, (0, 1, 0))
                    if t == 16 * u - 20:
                        write_split(u, QX, q_scr, q_high, q_low, q_out, (0, 0, 1))
                    if t == 16 * u - 19:
                        load_stack(2 * u)
                    if t == 16 * u - 18:
                        load_stack(2 * u + 1)
                    if t == 16 * u - 15:
                        masks_by_query(u)
                if t == -14:
                    sp.wait_ge(bias_ready, 2)
                    load(bias_scr[1:], BH[1].bitcast(F32), bias_out)
                for kind, v in SIDE.get(t - 1, ()):
                    if kind == "eT" and v < UNITS - 1:
                        f, n = filled("eT", v)
                        sp.wait_ge(f, n)
                        load(E[:], ctx_in[v - NB + 1].rearrange("(t p) d -> p t d", p=P), e_in)
                for i, (w, o, lot) in enumerate(PARTS[:-1]):
                    if t == SPLIT_STEPS[i] + 1 and PARTS[i + 1][2] > lot:
                        load_lot(lot + 1)
            for b in range(NB):
                sp.wait_ge(fin_done, b + 1)
                load(out[b].rearrange("(t p) d -> p t d", p=P), X[:, b], out_done)
            sp.wait_ge(out_done, 16 * NB)

        @block.gpsimd
        def _(pool):
            pool.memset(IDN[:], 0.0).then_inc(id_zero, 1)
            pool.wait_ge(id_zero, 1)
            pool.affine_select(out=IDN[:], in_=IDN[:], compare_op=ALU.not_equal, fill=1.0, base=0,
                               pattern=[[-1, P]], channel_multiplier=1).then_inc(const_ready, 1)
            pool.memset(NEGH[:], -0.5).then_inc(const_ready, 1)
            pool.memset(ONE, 1.0).then_inc(const_ready, 1)

            def set_stack(i):
                rows = slice(64 * i + 32, 64 * i + 64)
                pool.memset(QS[rows].bitcast(F32), 1.0).then_inc(stack_set, 1)
                pool.wait_ge(stack_set, 2 * i + 1)
                pool.memset(KS[rows].bitcast(F32), 1.0).then_inc(stack_set, 1)
                pool.wait_ge(stack_set, 2 * i + 2)

            def rstd(n):
                pool.wait_ge(mv_ready, n + 1)
                if n == 0:
                    pool.wait_ge(const_ready, 3)
                if n >= 2:
                    pool.wait_ge(xn_ready, n - 1)
                r = RS[:, n % 2, :]
                pool.tensor_scalar(r, MV[:, n % 2, :, 1], 1.0, EPS, ALU.mult, ALU.add).then_inc(rstd_step, 1)
                pool.wait_ge(rstd_step, n + 1)
                pool.tensor_tensor(r, r, NEGH[:], ALU.pow).then_inc(rstd_ready, 1)

            def residual_bias(kind, b):
                n = norm_index(kind, b)
                pool.wait_ge(xn_ready, n + 1)
                if n == 0:
                    pool.wait_ge(bvec_in, 16 * 3)
                bias = BO[:, {"xT": 0, "xT2": 1, "xT3": 2}[kind], :].unsqueeze(1).broadcast_to([P, TT, D])
                pool.tensor_tensor(X[:, b], X[:, b], bias, ALU.add).then_inc(resid_ready, 1)

            def low_of_norm(kind, b):
                dst = norm_dst(kind, b)
                pool.wait_ge(xt_high, norm_index(kind, b) + 1)
                pool.tensor_tensor(dst[1][:], XT32[:], dst[0][:].bitcast(F32), ALU.subtract).then_inc(xt_low, 1)

            def low_of_keys(u):
                pool.wait_ge(k_high, u + 1)
                pool.tensor_tensor(KX[:, 1], K32[:], KX[:, 0].bitcast(F32), ALU.subtract).then_inc(k_low, 1)

            pool.wait_ge(const_ready, 3)
            for t in range(FIRST_STEP, LAST_STEP + 1):
                for kind, b in STATS.get(t, ()):
                    rstd(norm_index(kind, b))
                for kind, u in SIDE.get(t - 2, ()):
                    if kind in ("xT", "xT2", "xT3"):
                        low_of_norm(kind, u)
                    if kind == "k":
                        low_of_keys(u)
                for kind, b in STATS.get(t - 2, ()):
                    residual_bias(kind, b)
                if t == -34:
                    pool.wait_ge(rstd_ready, 1)
                    set_stack(0)
                if t == -23:
                    pool.wait_ge(k_low, 1)
                    pool.memset(V[:, :, :, :, HD:], 1.0).then_inc(v_ones, 1)
                    pool.wait_ge(v_ones, 1)
                    set_stack(1)
                for i, (w, o, lot) in enumerate(PARTS):
                    if t == SPLIT_STEPS[i]:
                        pool.wait_ge(stg_high, i + 1)
                        pool.tensor_tensor(w[1], STG[:, o:o + 512], w[0].bitcast(F32), ALU.subtract).then_inc(stg_low, 1)

        @block.scalar
        def _(act):
            for (v, n), c in zip(vecs, col):
                act.dma_start(ROWV[c:c + n, :], v[0:n * P].rearrange("(r p) -> r p", p=P)).then_inc(vec_in, 16)
            for i, v in enumerate((b_ao, b_co, b2)):
                act.dma_start(BO[:, i, :], v.partition_broadcast(P)).then_inc(bvec_in, 16)

            def evacuate(kind, u):
                bank, n = side_slot(kind, u)
                tile = PSD[:, bank, :]
                if kind in ("xT", "xT2", "xT3"):
                    i = norm_index(kind, u)
                    act.wait_ge(side_filled[bank], n + 1)
                    if i:
                        act.wait_ge(xt_low, i)
                    else:
                        act.wait_ge(cols_ready, 1)
                    cs, cb = C_NORM[kind]
                    for c in range(KC):
                        m = act.activation(XT32[:, c, :], tile[:, c * S:(c + 1) * S], ACT.Identity,
                                           scale=COLV[:, cs + c:cs + c + 1], bias=COLV[:, cb + c:cb + c + 1])
                    m.then_inc(xt32_ready, 1)
                if kind == "eT":
                    act.wait_ge(side_filled[bank], n + 1)
                    act.wait_ge(*filled("v", u - 1))
                    act.activation(XS[0][:].rearrange("p c n -> p (c n)"), tile, ACT.Copy).then_inc(e_high, 1)
                if kind == "q":
                    act.wait_ge(side_filled[bank], n + 1)
                    if u:
                        act.wait_ge(q_out, 48 * u)
                    cq = C_Q[u // NB]
                    for c in range(2):
                        m = act.activation(QX[:, 0, c, :], tile[:, c * S:(c + 1) * S], ACT.Identity,
                                           bias=COLV[:, cq + c:cq + c + 1])
                    m.then_inc(q_high, 1)
                if kind == "v":
                    act.wait_ge(side_filled[bank], n + 1)
                    if u >= 2:
                        act.wait_ge(pv_done, 4 * (u - 1))
                    act.activation(V[:, u % 2, :, :, 0:HD], tile.rearrange("p (t h d) -> p t h d", t=TT, h=NH),
                                   ACT.Copy).then_inc(v_ready, 1)
                if kind == "maxT":
                    s, j, n_ = u, mask_of(u // 2), u % 2
                    act.wait_ge(side_filled[bank], n + 1)
                    act.wait_ge(flags_ready, flags_count(s // 2))
                    act.reg_load(m_flag, FLG[0:1, j:j + 1].bitcast(I32))
                    with act.If_ne(m_flag, 0):
                        if n_:
                            act.wait_ge(g_max_out[s // 2], 16)
                        act.activation(CG[:], tile[0:HH, 0:S], ACT.Copy, scale=-1.0).then_inc(g_max_ready[s // 2], 1)
                        act.wait_ge(g_max_ready[s // 2], n_ + 1)
                        act.dma_start(max_scr[s], CG[:, :]).then_inc(g_max_out[s // 2], 16)
                    if s >= 2:
                        act.wait_ge(crow_in, 16 * (s - 1))
                    act.activation(CR[:, n_, :], tile[0:HH, 0:S], ACT.Copy, scale=NFR[0:HH, j:j + 1]).then_inc(crow_ready, 1)
                    act.wait_ge(crow_ready, s + 1)
                    act.dma_start(stack_rows(QS, s, CROW, CROW + 1).bitcast(F32), CR[:, n_, :].bitcast(F32)).then_inc(
                        crow_in, 16)
                if kind == "up" and u < EARLY:
                    act.wait_ge(side_filled[bank], n + 1)
                    act.wait_ge(bias_out, 32)
                    for c in range(2):
                        k = C_B1 + 2 * (u % 4) + c
                        m = act.activation(PRE[:, u, c, :].bitcast(F32), tile[:, c * S:(c + 1) * S], ACT.Identity,
                                           bias=COLV[:, k:k + 1])
                    m.then_inc(pre_ready, 1)
                if kind == "ctxT":
                    act.wait_ge(side_filled[bank], n + 1)
                    if u:
                        act.wait_ge(*filled("o", u - 1))
                    cv = C_V[u // NB]
                    for c in range(KC):
                        m = act.activation(CX[0][:, c, :], tile[:, c * S:(c + 1) * S], ACT.Identity,
                                           bias=COLV[:, cv + c:cv + c + 1])
                    m.then_inc(cx_high, 1)

            def gelu(m_):
                bank, n = side_slot("up", m_)
                if m_ < EARLY:
                    src = PRE[:, m_].bitcast(F32)
                    act.wait_ge(pre_ready, m_ + 1)
                else:
                    src = PSD[:, bank, :].rearrange("p (c n) -> p c n", c=2)
                    act.wait_ge(side_filled[bank], n + 1)
                if m_ >= 2:
                    act.wait_ge(hid_low, m_ - 1)
                else:
                    act.wait_ge(stg_low, len(PARTS))
                for c in range(2):
                    k = C_B1 + 2 * (m_ % 4) + c
                    m = act.activation(G32[:, m_ % 2, c * S:(c + 1) * S], src[:, c, :], ACT.Gelu_apprx_tanh,
                                       bias=0.0 if m_ < EARLY else COLV[:, k:k + 1])
                m.then_inc(gelu_done, 1)

            def high_of_keys(u):
                act.wait_ge(k32_ready, u + 1)
                if u:
                    act.wait_ge(k_out, 48 * u)
                act.activation(KX[:, 0], K32[:], ACT.Copy).then_inc(k_high, 1)

            flag = act.alloc_register("act_flag")
            m_flag = act.alloc_register("act_m_flag")

            def spread_maxima(s):
                u, n = s // 2, s % 2
                with act.If_ne(flag, 0):
                    act.wait_ge(g_max_out[u], 16 * (n + 1))
                    if s:
                        act.wait_ge(exp_done, 8 * s)
                    act.dma_start(CB[:], max_scr[s].partition_broadcast(P)).then_inc(g_bcast_in[u], 16)
                    if n == 0:
                        with nc.allow_non_contiguous_dma(reason="transposed mask, only on this path"):
                            for t in range(TT):
                                act.dma_start(MGT[:, t], mask_dram(mask_of(u))[:, t * P:(t + 1) * P].rearrange(
                                    "q p -> p q")).then_inc(g_mask_in[u], 16)

            def exps(t):
                g, kt, hp, u = t // 4, (t % 4) // 2, t % 2, t // 16
                if t % 16 == 0:
                    act.wait_ge(flags_ready, flags_count(u))
                    act.reg_load(flag, FLG[0:1, mask_of(u):mask_of(u) + 1].bitcast(I32))
                if t % 8 == 0:
                    spread_maxima(t // 8)
                act.wait_ge(b_ready, t + 1)
                with act.If_ne(flag, 0):
                    act.wait_ge(g_fixed[u], t % 16 + 1)
                if t % 4 == 0 and g >= 2:
                    act.wait_ge(pv_done, g - 1)
                if t == 0:
                    act.wait_ge(wqkv_split, 2)
                    act.wait_ge(mask_dif, 2)
                act.activation(PR[:, g % 2, kt, 2 * hp:2 * hp + 2, :],
                               PB[:, t % 2, :].rearrange("p (h n) -> p h n", h=2),
                               ACT.Exp, scale=SCORE_SCALE).then_inc(exp_done, 1)

            def context_out(g):
                act.wait_ge(pv_done, g + 1)
                if g:
                    act.wait_ge(ot_done, g)
                act.activation(O32[:], PV[:, g % 2, 0:S], ACT.Copy).then_inc(o_ready, 1)

            for t in range(FIRST_STEP, LAST_STEP + 1):
                for kind, u in SIDE.get(t - 1, ()):
                    evacuate(kind, u)
                if 0 <= t < CHUNKS:
                    exps(t)
                if t % 4 == 2 and 0 <= (t - 6) // 4 < GROUPS:
                    context_out((t - 6) // 4)
                for m_ in range(PIECES):
                    if t == GELU_STEPS[m_]:
                        gelu(m_)
                for kind, u in SIDE.get(t - 2, ()):
                    if kind == "k":
                        high_of_keys(u)
                for i, (w, o, lot) in enumerate(PARTS):
                    if t == SPLIT_STEPS[i]:
                        act.wait_ge(stg_in, 16 * (lot + 2))
                        act.activation(w[0], STG[:, o:o + 512], ACT.Copy).then_inc(stg_high, 1)

        @block.vector
        def _(dve):
            def split_wqkv():
                dve.wait_ge(wqkv_in, 16)
                dve.tensor_copy(WQKV[0][:], RAWQKV).then_inc(wqkv_split, 1)
                dve.wait_ge(wqkv_split, 1)
                dve.tensor_tensor(WQKV[1][:], RAWQKV, WQKV[0][:].bitcast(F32), ALU.subtract).then_inc(wqkv_split, 1)

            def mask_difference(i, lo, hi):
                dve.wait_ge(mask0_in if i == 0 else masks_in, 32)
                dve.tensor_tensor(MK[:, lo:hi], MK[:, lo:hi], MB[:, lo:hi, :].unsqueeze(2).broadcast_to([P, hi - lo, TT, S]),
                                  ALU.not_equal).then_inc(mask_step, 1)
                dve.wait_ge(mask_step, i + 1)
                dve.tensor_reduce(DIF[:, lo:hi], MK[:, lo:hi].rearrange("p j t n -> p j (t n)"), AX.X,
                                  ALU.add).then_inc(mask_dif, 1)

            def mask_flags(i, lo, hi):
                bank, n = side_slot("flags", i)
                dve.wait_ge(side_filled[bank], n + 1)
                k = 5 * i
                dve.tensor_scalar(FLG[:, lo:hi], PSD[:, bank, 0:hi - lo], 1.0, None, ALU.min).then_inc(flag_step, 1)
                dve.wait_ge(flag_step, k + 1)
                dve.tensor_scalar(FLR[:, lo:hi], FLG[:, lo:hi], -1.0, 1.0, ALU.mult, ALU.add).then_inc(flag_step, 1)
                dve.wait_ge(flag_step, k + 2)
                for j in range(lo, hi):
                    m = dve.tensor_scalar(MB[:, j, :], MB[:, j, :], FLR[:, j:j + 1], FLG[:, j:j + 1], ALU.mult, ALU.add)
                m.then_inc(flag_step, 1)
                dve.wait_ge(flag_step, k + 3)
                if i:
                    dve.wait_ge(bias_ready, 1)
                dve.tensor_scalar(BF[:, 0:hi - lo], MB[0:1, lo:hi], -1.0, BIAS, ALU.add, ALU.mult).then_inc(flag_step, 1)
                dve.wait_ge(flag_step, k + 4)
                dve.tensor_copy(BH[i][:, :, 0, :], BF[:, 0:hi - lo]).then_inc(flag_step, 1)
                dve.wait_ge(flag_step, k + 5)
                dve.tensor_tensor(BH[i][:, :, 1, :], BF[:, 0:hi - lo], BH[i][:, :, 0, :].bitcast(F32),
                                  ALU.subtract).then_inc(bias_ready, 1)
                dve.tensor_scalar(NFR[:, lo:hi], FLG[:, lo:hi], -1.0, None, ALU.add).then_inc(flags_ready, 1)

            def norm_stats(kind, b):
                n = norm_index(kind, b)
                if kind == "xT":
                    dve.wait_ge(x_in[b], 16)
                else:
                    dve.wait_ge(o_added, b + 1 + (NB if kind == "xT3" else 0))
                for t in range(TT):
                    m = dve.bn_stats(ST[:, n % 2, t, :], X[:, b, t, :])
                m.then_inc(stats_ready, 1)
                dve.wait_ge(stats_ready, n + 1)
                if n >= 2:
                    dve.wait_ge(xn_ready, n - 1)
                for t in range(TT):
                    m = dve.bn_aggr(MV[:, n % 2, t, :], ST[:, n % 2, t, :])
                m.then_inc(mv_ready, 1)

            def normalise(kind, b):
                n = norm_index(kind, b)
                dve.wait_ge(rstd_ready, n + 1)
                if n:
                    dve.wait_ge(*filled(*NORMS[n - 1]))
                for t in range(TT):
                    m = dve.tensor_scalar(XN[:, t, :], X[:, b, t, :], MV[:, n % 2, t, 0:1], RS[:, n % 2, t:t + 1],
                                          ALU.subtract, ALU.mult)
                m.then_inc(xn_ready, 1)

            a_flag = dve.alloc_register("a_flag")
            b_flag = dve.alloc_register("b_flag")

            def evacuate(kind, u):
                bank, n = side_slot(kind, u)
                tile = PSD[:, bank, :]
                if kind in ("cols", "k", "o"):
                    dve.wait_ge(side_filled[bank], n + 1)
                if kind == "cols":
                    dve.tensor_copy(COLV[:, 0:NV], tile[:, 0:NV]).then_inc(cols_ready, 1)
                if kind == "flags":
                    mask_flags(u, *((0, 1) if u == 0 else (1, 1 + NB)))
                if kind == "k":
                    if u:
                        dve.wait_ge(k_low, u)
                    else:
                        dve.wait_ge(cols_ready, 1)
                    if u in (0, NB):
                        dve.wait_ge(flag_step, 5 * (u // NB) + 3)
                    ck = C_K[u // NB]
                    for c in range(2):
                        m = dve.scalar_tensor_tensor(K32[:, c, :], tile[:, c * S:(c + 1) * S], COLV[:, ck + c:ck + c + 1],
                                                     MB[:, mask_of(u), :], ALU.add, ALU.mult)
                    m.then_inc(k32_ready, 1)
                if kind == "o":
                    b = u % NB
                    dve.wait_ge(resid_ready, norm_index("xT" if u < NB else "xT2", b) + 1)
                    xb = X[:, b].rearrange("p t d -> p (t d)")
                    dve.tensor_tensor(xb, xb, tile, ALU.add).then_inc(o_added, 1)

            def split(kind, u):
                bank, n = side_slot(kind, u)
                tile = PSD[:, bank, :]
                if kind in ("xT", "xT2", "xT3"):
                    dve.wait_ge(xt32_ready, norm_index(kind, u) + 1)
                    if norm_dst_used(kind, u):
                        dve.wait_ge(*filled(*norm_dst_used(kind, u)))
                    dve.tensor_copy(norm_dst(kind, u)[0][:], XT32[:]).then_inc(xt_high, 1)
                if kind == "eT":
                    dve.wait_ge(e_high, u - NB + 1)
                    dve.tensor_tensor(XS[1][:].rearrange("p c n -> p (c n)"), tile,
                                      XS[0][:].bitcast(F32).rearrange("p c n -> p (c n)"), ALU.subtract).then_inc(e_low, 1)
                if kind == "q":
                    dve.wait_ge(q_high, u + 1)
                    cq = C_Q[u // NB]
                    for c in range(2):
                        m = dve.scalar_tensor_tensor(QX[:, 1, c, :], tile[:, c * S:(c + 1) * S], COLV[:, cq + c:cq + c + 1],
                                                     QX[:, 0, c, :].bitcast(F32), ALU.add, ALU.subtract)
                    m.then_inc(q_low, 1)
                if kind == "ctxT":
                    dve.wait_ge(cx_high, u + 1)
                    cv = C_V[u // NB]
                    for c in range(KC):
                        m = dve.scalar_tensor_tensor(CX[1][:, c, :], tile[:, c * S:(c + 1) * S], COLV[:, cv + c:cv + c + 1],
                                                     CX[0][:, c, :].bitcast(F32), ALU.add, ALU.subtract)
                    m.then_inc(cx_low, 1)

            def split_hidden(m_):
                hid, c2 = HID[m_ // 4 % 2], 2 * (m_ % 4)
                dve.wait_ge(gelu_done, m_ + 1)
                if m_ >= 8:
                    dve.wait_ge(down_done, m_ - 7)
                else:
                    dve.wait_ge(b_ready, CHUNKS)
                g = G32[:, m_ % 2, :].rearrange("p (c n) -> p c n", c=2)
                dve.tensor_copy(hid[0][:, c2:c2 + 2, :], g).then_inc(hid_high, 1)
                dve.wait_ge(hid_high, m_ + 1)
                dve.tensor_tensor(hid[1][:, c2:c2 + 2, :], g, hid[0][:, c2:c2 + 2, :].bitcast(F32),
                                  ALU.subtract).then_inc(hid_low, 1)

            def maxima(a):
                s, i, u = a // 8, a % 8, a // 16
                qt, hp = i // 4, i % 4
                j, k = mask_of(u), 3 * (a % 16)
                if a % 16 == 0:
                    dve.wait_ge(flags_ready, flags_count(u))
                    dve.reg_load(a_flag, FLG[0:1, j:j + 1].bitcast(I32))
                dve.wait_ge(a_ready, a + 1)
                tile = PA[:, a % 2, :].rearrange("p (h n) -> p h n", h=2)
                with dve.If_ne(a_flag, 0):
                    if a % 16 == 0:
                        dve.wait_ge(g_mask_in[u], 16)
                    dve.tensor_scalar(MBI[:, 0, :], MG[:, qt, :], -1.0, BIAS, ALU.add, ALU.mult).then_inc(g_step_a[u], 1)
                    dve.tensor_tensor(tile, tile, MG[:, qt, :].unsqueeze(1).broadcast_to([P, 2, S]),
                                      ALU.mult).then_inc(g_step_a[u], 1)
                    dve.wait_ge(g_step_a[u], k + 2)
                    dve.tensor_tensor(tile, tile, MBI[:, 0, :].unsqueeze(1).broadcast_to([P, 2, S]),
                                      ALU.add).then_inc(g_step_a[u], 1)
                    dve.wait_ge(g_step_a[u], k + 3)
                if i == 0 and s >= 2:
                    dve.wait_ge(*filled("maxT", s - 2))
                dve.tensor_reduce(MX[:, s % 2, qt, 2 * hp:2 * hp + 2], tile, AX.X, ALU.max).then_inc(max_done, 1)

            def mask_scores(t):
                s, i, u = t // 8, t % 8, t // 16
                kt, h0 = (i % 4) // 2, 4 * (i // 4) + 2 * (i % 2)
                j, k = mask_of(u), 3 * (t % 16)
                if t % 16 == 0:
                    dve.reg_load(b_flag, FLG[0:1, j:j + 1].bitcast(I32))
                with dve.If_ne(b_flag, 0):
                    dve.wait_ge(b_ready, t + 1)
                    if i == 0:
                        dve.wait_ge(g_mask_in[u], 16 * (1 + TT))
                        dve.wait_ge(g_bcast_in[u], 16 * (s % 2 + 1))
                    tile = PB[:, t % 2, :].rearrange("p (h n) -> p h n", h=2)
                    dve.tensor_scalar(MBI[:, 1, :], MGT[:, kt, :], -1.0, BIAS, ALU.add, ALU.mult).then_inc(g_step_b[u], 1)
                    dve.tensor_tensor(tile, tile, MGT[:, kt, :].unsqueeze(1).broadcast_to([P, 2, S]),
                                      ALU.mult).then_inc(g_step_b[u], 1)
                    dve.wait_ge(g_step_b[u], k + 2)
                    dve.tensor_tensor(tile, tile, MBI[:, 1, :].unsqueeze(1).broadcast_to([P, 2, S]),
                                      ALU.add).then_inc(g_step_b[u], 1)
                    dve.wait_ge(g_step_b[u], k + 3)
                    dve.tensor_tensor(tile, tile, CB[:, h0:h0 + 2, :], ALU.add).then_inc(g_fixed[u], 1)
                    dve.wait_ge(g_fixed[u], t % 16 + 1)

            def normalise_context(g):
                u, r = g // 4, g % 2
                dve.wait_ge(ot_done, g + 1)
                src = PV[:, r, S:2 * S].rearrange("p (th w) -> p th w", w=2 * HD)
                dve.reciprocal(RC[:, r, :], src[:, :, HD]).then_inc(recip_done, 1)
                dve.wait_ge(recip_done, g + 1)
                if g % 4 == 0 and u:
                    dve.wait_ge(*filled("ctxT", u - 1))
                h = (g % 4) * 4 * HD
                dve.tensor_tensor(CT[:, :, h:h + 4 * HD].rearrange("p t (h d) -> p t h d", h=4),
                                  src.rearrange("p (t h) w -> p t h w", t=TT)[:, :, :, 0:HD],
                                  RC[:, r, :].rearrange("p (t h) -> p t h", t=TT).unsqueeze(3)
                                  .broadcast_to([P, TT, 4, HD]), ALU.mult).then_inc(ctx_done, 1)

            def finish(b):
                acc = MLP_OUT[b]
                dve.wait_ge(down_done, 4 * b + 4)
                dve.wait_ge(resid_ready, norm_index("xT3", b) + 1)
                dve.tensor_tensor(X[:, b], X[:, b], acc[:, :, 0:D], ALU.add).then_inc(fin_done, 1)

            for t in range(FIRST_STEP, LAST_STEP + 1):
                for kind, u in SIDE.get(t - 1, ()):
                    evacuate(kind, u)
                if 0 <= t + LEAD < CHUNKS:
                    maxima(t + LEAD)
                if 0 <= t < CHUNKS:
                    mask_scores(t)
                for kind, u in SIDE.get(t - 2, ()):
                    split(kind, u)
                if t % 4 == 1 and 0 <= (t - 9) // 4 < GROUPS:
                    normalise_context((t - 9) // 4)
                for kind, b in STATS.get(t - 2, ()):
                    normalise(kind, b)
                for kind, b in STATS.get(t, ()):
                    norm_stats(kind, b)
                if t == -32:
                    split_wqkv()
                if t == -30:
                    mask_difference(0, 0, 1)
                if t == -20:
                    mask_difference(1, 1, 1 + NB)
                for m_ in range(PIECES):
                    if t == GELU_STEPS[m_] + 1:
                        split_hidden(m_)
                    if m_ % 4 == 3 and t == DOWN_STEPS[m_] + 1:
                        finish(m_ // 4)

        @block.tensor
        def _(pe):
            def three(dst, lhs, rhs, first, last):
                pe.matmul(dst, lhs[0], rhs[0], start=first, stop=False)
                pe.matmul(dst, lhs[0], rhs[1], start=False, stop=False)
                return pe.matmul(dst, lhs[1], rhs[0], start=False, stop=last)

            def project_cols(tile, w, lo, src, chunks):
                for c in chunks:
                    for k in range(KC):
                        o = lo + c * P
                        m = three(tile[:, c * S:(c + 1) * S], [t[:, k, o:o + P] for t in w], [t[:, k, :] for t in src],
                                  k == 0, k == KC - 1)
                return m

            def project_rows(tile, src, w, lo, tiles):
                for t in tiles:
                    for k in range(KC):
                        m = three(tile[:, t * D:(t + 1) * D], [s[:, k, t * P:(t + 1) * P] for s in src],
                                  [v[:, k, lo:lo + D] for v in w], k == 0, k == KC - 1)
                return m

            def transpose_rows(tile, src):
                for k in range(KC):
                    for t in range(TT):
                        o = k * S + t * P
                        m = pe.transpose(tile[:, o:o + P], src[:, t, k * P:(k + 1) * P], IDN[:])
                return m

            def wait_for_bank(kind, u):
                j = SIDE_ORDER.index((kind, u))
                if j >= 2:
                    pe.wait_ge(*drained(*SIDE_ORDER[j - 2]))

            def projection(kind, u, half):
                bank, n = side_slot(kind, u)
                tile = PSD[:, bank, :]
                if half == 0:
                    wait_for_bank(kind, u)
                if kind == "k":
                    if half == 0 and u < NB:
                        pe.wait_ge(xt_low, norm_index("xT", u) + 1)
                        if u == 0:
                            pe.wait_ge(wqkv_split, 2)
                    elif half == 0:
                        pe.wait_ge(e_low, u - NB + 1)
                        pe.wait_ge(stg_low, W_KV_DONE)
                    m = project_cols(tile, *((WQKV, D) if u < NB else (WKV, 0)), XS, (half,))
                elif kind == "q":
                    if half == 0 and u >= NB:
                        pe.wait_ge(xt_low, norm_index("xT2", u - NB) + 1)
                        pe.wait_ge(stg_low, W_QUERY_DONE)
                    m = project_cols(tile, *((WQKV, 0, XS) if u < NB else (WQ, 0, XC)), (half,))
                elif kind == "up":
                    b = u // 4
                    if half == 0 and u % 4 == 0:
                        pe.wait_ge(xt_low, norm_index("xT3", b) + 1)
                        pe.wait_ge(stg_low, W_MLP_DONE)
                    m = project_cols(tile, W1, 2 * P * (u % 4), norm_dst("xT3", b), (half,))
                elif kind == "v":
                    m = project_rows(tile, XS, *((WQKV, 2 * D) if u < NB else (WKV, D)), (half,))
                else:
                    if half == 0:
                        pe.wait_ge(cx_low, u + 1)
                        pe.wait_ge(stg_low, W_AO_DONE if u < NB else W_CO_DONE)
                    m = project_rows(tile, CX, WAO if u < NB else WCO, 0, (half,))
                if half == 1:
                    m.then_inc(side_filled[bank], 1)

            def side(kind, u):
                bank, n = side_slot(kind, u)
                tile = PSD[:, bank, :]
                wait_for_bank(kind, u)
                if kind == "cols":
                    pe.wait_ge(const_ready, 3)
                    pe.wait_ge(vec_in, 16 * len(vecs))
                    m = pe.transpose(tile[:, 0:NV], ROWV[0:NV, :], IDN[0:NV, 0:NV])
                elif kind == "flags":
                    lo, hi = (0, 1) if u == 0 else (1, 1 + NB)
                    pe.wait_ge(mask_dif, u + 1)
                    m = pe.matmul(tile[:, 0:hi - lo], ONE, DIF[:, lo:hi], start=True, stop=True)
                elif kind in ("xT", "xT2", "xT3"):
                    pe.wait_ge(xn_ready, norm_index(kind, u) + 1)
                    m = transpose_rows(tile, XN)
                elif kind == "eT":
                    pe.wait_ge(e_in, 16 * (u - NB + 1))
                    m = transpose_rows(tile, E)
                elif kind == "maxT":
                    pe.wait_ge(max_done, 8 * u + 8)
                    for t in range(TT):
                        m = pe.transpose(tile[0:HH, t * P:(t + 1) * P], MX[:, u % 2, t, :], IDN[:])
                elif kind == "ctxT":
                    pe.wait_ge(ctx_done, 4 * u + 4)
                    m = transpose_rows(tile, CT)
                m.then_inc(side_filled[bank], 1)

            def scores_for_maxima(a):
                s, i = a // 8, a % 8
                r, qt, hp = s % RING, i // 4, i % 4
                queries, keys = stack_rows(QS, s, 0, ROWS_A), stack_rows(KS, s, 0, ROWS_A)
                if i == 0:
                    pe.wait_ge(stacked[r], stack_count(s))
                if a >= 2:
                    pe.wait_ge(max_done, a - 1)
                for n in range(2):
                    h = 2 * hp + n
                    m = pe.matmul(PA[:, a % 2, n * S:(n + 1) * S], queries[:, h, qt * P:(qt + 1) * P],
                                  keys[:, h, :], start=True, stop=True)
                m.then_inc(a_ready, 1)

            def scores_for_exp(t):
                s, i = t // 8, t % 8
                kt, h0 = (i % 4) // 2, 4 * (i // 4) + 2 * (i % 2)
                queries, keys = stack_rows(QS, s, 0, ROWS_B), stack_rows(KS, s, 0, ROWS_B)
                if i == 0:
                    pe.wait_ge(crow_in, 16 * (s + 1))
                if t >= 2:
                    pe.wait_ge(exp_done, t - 1)
                for n in range(2):
                    m = pe.matmul(PB[:, t % 2, n * S:(n + 1) * S], keys[:, h0 + n, kt * P:(kt + 1) * P],
                                  queries[:, h0 + n, :], start=True, stop=True)
                m.then_inc(b_ready, 1)

            def context(g):
                u, r = g // 4, g % 2
                pe.wait_ge(exp_done, 4 * g + 4)
                if g % 4 == 0:
                    pe.wait_ge(v_ready, u + 1)
                    pe.wait_ge(v_ones, 1)
                if g >= 2:
                    pe.wait_ge(ctx_done, g - 1)
                for kt in range(TT):
                    for n in range(4):
                        m = pe.matmul(PV[32 * n:32 * n + 32, r, 0:S], V[:, u % 2, kt, 4 * (g % 4) + n, :],
                                      PR[:, r, kt, n, :], start=(kt == 0), stop=(kt == TT - 1),
                                      tile_position=(0, 32 * n))
                m.then_inc(pv_done, 1)

            def transpose_context(g):
                r = g % 2
                pe.wait_ge(o_ready, g + 1)
                for t in range(TT):
                    m = pe.transpose(PV[:, r, S + t * P:S + (t + 1) * P], O32[:, t * P:(t + 1) * P], IDN[:])
                m.then_inc(ot_done, 1)

            def down(m_):
                b, c = m_ // 4, m_ % 4
                acc = MLP_OUT[b]
                pe.wait_ge(hid_low, m_ + 1)
                if c == 0:
                    pe.wait_ge(*((max_done, CHUNKS), (exp_done, CHUNKS), (fin_done, 1), (fin_done, 2))[b])
                for t in range(TT):
                    for k in (2 * c, 2 * c + 1):
                        m = three(acc[:, t, 0:D], [h[:, k, t * P:(t + 1) * P] for h in HID[b % 2]], [w[:, k, :] for w in W2],
                                  k == 0, k == FC - 1)
                m.then_inc(down_done, 1)

            for t in range(FIRST_STEP, LAST_STEP + 1):
                if 0 <= t + LEAD < CHUNKS:
                    scores_for_maxima(t + LEAD)
                if 0 <= t < CHUNKS:
                    scores_for_exp(t)
                if t % 4 == 1 and 0 <= (t - 5) // 4 < GROUPS:
                    context((t - 5) // 4)
                if t % 4 == 0 and 0 <= (t - 8) // 4 < GROUPS:
                    transpose_context((t - 8) // 4)
                for kind, u in SIDE.get(t, ()):
                    if kind in HALVED:
                        projection(kind, u, 1)
                    else:
                        side(kind, u)
                for kind, u in SIDE.get(t + 1, ()):
                    if kind in HALVED:
                        projection(kind, u, 0)
                if t in DOWN_STEPS:
                    down(DOWN_STEPS.index(t))


_INS = ["x", "ctx_2048", "mask_1x1xSxS2_fc1", "mask_Bx1xSxS2_ff1"] + ["L0_xattn_" + n for n in (
    "ln1_s", "ln1_b", "w_qkv", "b_qkv", "w_ao", "b_ao", "ln2_s", "ln2_b", "w_q", "b_q", "w_kv", "b_kv",
    "w_co", "b_co", "ln3_s", "ln3_b", "w1", "b1", "w2", "b2")]


def kernel(**inputs):
    import numpy as _np
    import concourse.bacc as _bacc
    from concourse import mybir as _mybir
    from concourse.bass_utils import run_bass_kernel_spmd as _run

    nc = _bacc.Bacc("TRN2", target_bir_lowering=False, num_devices=1)
    arrays, args = {}, []
    for name in _INS:
        a = _np.ascontiguousarray(inputs[name])
        arrays[f"in_{name}_dram"] = a
        args.append(nc.dram_tensor(f"in_{name}_dram", a.shape, _mybir.dt.from_np(a.dtype), kind="ExternalInput").ap())
    args.append(nc.dram_tensor("out_0_dram", (NB, S, D), _mybir.dt.float32, kind="ExternalOutput").ap())
    decoder_layer(nc, *args)
    r = _run(nc, [arrays], core_ids=[0])
    return r.results[0]["out_0_dram"]
```
